# Optimizing a Trainium2 kernel written in Bass

```python
import numpy as np
import jax
import jax.numpy as jnp

def _softmax(x, axis=-1):
    return jax.nn.softmax(x, axis=axis)

def _gelu(x):
    return jax.nn.gelu(x, approximate=True)

def _silu(x):
    return jax.nn.silu(x)

def _sigmoid(x):
    return jax.nn.sigmoid(x)

def _layernorm(x, axis=-1, eps=1e-05):
    m = jnp.mean(x, axis=axis, keepdims=True)
    v = jnp.var(x, axis=axis, keepdims=True)
    return (x - m) / jnp.sqrt(v + eps)

def _scatter_add(tgt, idx, src, axis=0):
    return tgt.at[idx].add(src)

def _segment_sum(src, seg, n):
    return jax.ops.segment_sum(src, seg, n)
kernel_name = 'mk_cond_resid_d2_seqx_r2_b3b03e'

def setup_inputs(seed: int=0):
    np.random.seed(seed)
    _w = jnp.asarray

    def _rec_inputs():
        import jax
        import jax.numpy as jnp
        _rk = jax.random.key(seed)
        x = 7.22e-05 + 1 * jax.random.normal(jax.random.fold_in(_rk, 1), (8, 512, 512), jnp.float32)
        _lenS = 512 - jax.random.randint(jax.random.fold_in(_rk, 7), (8,), 0, max(1, 512 // 4) + 1, jnp.int32)
        _lenS2 = 512 - jax.random.randint(jax.random.fold_in(_rk, 8), (8,), 0, max(1, 512 // 4) + 1, jnp.int32)
        fside_BxSxS_0 = 4.13588e-05 + 0.999923 * jax.random.normal(jax.random.fold_in(_rk, 11), (8, 512, 512), jnp.float32)
        itok_B_18_1004 = jax.random.randint(jax.random.fold_in(_rk, 12), (8,), 18, 1005, jnp.int32)
        itok_B_0_7 = jax.random.randint(jax.random.fold_in(_rk, 13), (8,), 0, 8, jnp.int32)
        return (x, fside_BxSxS_0, itok_B_18_1004, itok_B_0_7)
    x, fside_BxSxS_0, itok_B_18_1004, itok_B_0_7 = _rec_inputs()

    def _L0_cond_setup():
        import jax, jax.numpy as jnp
        import numpy as np
        B, L1, L2, DIN, DOUT, H = (8, 512, 512, 512, 512, 16)
        DH = DOUT // H
        SCALE = 1.0 / np.sqrt(DH).astype(np.float32)
        key = jax.random.key(seed)
        ks = jax.random.split(key, 13)
        s = 0.02
        return {'seq1': jax.random.normal(ks[0], (B, L1, DIN), jnp.float32), 'seq2': jax.random.normal(ks[1], (B, L2, DIN), jnp.float32), 'seq_len1': jax.random.randint(ks[2], (B,), 1, L1 + 1, jnp.int32), 'Wq': jax.random.normal(ks[3], (DIN, DOUT), jnp.float32) * s, 'bq': jnp.zeros((DOUT,), jnp.float32), 'Wk': jax.random.normal(ks[4], (DIN, DOUT), jnp.float32) * s, 'bk': jnp.zeros((DOUT,), jnp.float32), 'Wv': jax.random.normal(ks[5], (DIN, DOUT), jnp.float32) * s, 'bv': jnp.zeros((DOUT,), jnp.float32), 'Wo': jax.random.normal(ks[6], (DOUT, DOUT), jnp.float32) * s, 'bo': jnp.zeros((DOUT,), jnp.float32), 'b_prev': jax.random.normal(ks[7], (1, 1, DIN), jnp.float32) * s, 'b_self': jax.random.normal(ks[8], (1, 1, DIN), jnp.float32) * s}
    _L0_cond_all = _L0_cond_setup()
    _L0_cond_in = {k: v for k, v in _L0_cond_all.items() if k in ('Wq', 'bq', 'Wk', 'bk', 'Wv', 'bv', 'Wo', 'bo', 'b_prev', 'b_self')}
    del _L0_cond_all

    def _L1_cond_setup():
        import jax, jax.numpy as jnp
        import numpy as np
        IN, HID, OUT, PART, E = (512, 2048, 512, 128, 8)
        B, N = (16, 1024)
        key = jax.random.key(seed)
        ks = jax.random.split(key, 8)
        s1 = 1.0 / np.sqrt(IN)
        s2 = 1.0 / np.sqrt(HID)
        return {'x': jax.random.normal(ks[0], (B, N, IN), dtype=jnp.float32), 'indices': jax.random.randint(ks[1], (B,), 0, E, dtype=jnp.int64), 'W1': jax.random.uniform(ks[2], (IN, HID), jnp.float32, -s1, s1), 'b1': jax.random.uniform(ks[3], (HID,), jnp.float32, -s1, s1), 'W2': jax.random.uniform(ks[4], (HID, OUT - PART), jnp.float32, -s2, s2), 'b2': jax.random.uniform(ks[5], (OUT - PART,), jnp.float32, -s2, s2), 'We': jax.random.uniform(ks[6], (E, HID, PART), jnp.float32, -s2, s2), 'be': jax.random.uniform(ks[7], (E, PART), jnp.float32, -s2, s2)}
    _L1_cond_all = _L1_cond_setup()
    _L1_cond_in = {k: v for k, v in _L1_cond_all.items() if k in ('W1', 'b1', 'W2', 'b2', 'We', 'be')}
    del _L1_cond_all
    return {'x': x, 'fside_BxSxS_0': fside_BxSxS_0, 'itok_B_18_1004': itok_B_18_1004, 'itok_B_0_7': itok_B_0_7, 'L0_cond_Wq': _L0_cond_in['Wq'], 'L0_cond_bq': _L0_cond_in['bq'], 'L0_cond_Wk': _L0_cond_in['Wk'], 'L0_cond_bk': _L0_cond_in['bk'], 'L0_cond_Wv': _L0_cond_in['Wv'], 'L0_cond_bv': _L0_cond_in['bv'], 'L0_cond_Wo': _L0_cond_in['Wo'], 'L0_cond_bo': _L0_cond_in['bo'], 'L0_cond_b_prev': _L0_cond_in['b_prev'], 'L0_cond_b_self': _L0_cond_in['b_self'], 'L1_cond_W1': _L1_cond_in['W1'], 'L1_cond_b1': _L1_cond_in['b1'], 'L1_cond_W2': _L1_cond_in['W2'], 'L1_cond_b2': _L1_cond_in['b2'], 'L1_cond_We': _L1_cond_in['We'], 'L1_cond_be': _L1_cond_in['be']}

def reference(x, fside_BxSxS_0, itok_B_18_1004, itok_B_0_7, L0_cond_Wq, L0_cond_bq, L0_cond_Wk, L0_cond_bk, L0_cond_Wv, L0_cond_bv, L0_cond_Wo, L0_cond_bo, L0_cond_b_prev, L0_cond_b_self, L1_cond_W1, L1_cond_b1, L1_cond_W2, L1_cond_b2, L1_cond_We, L1_cond_be):
    import jax
    import jax.numpy as jnp

    def _L0_cond_ref(seq1, seq2, seq_len1, Wq, bq, Wk, bk, Wv, bv, Wo, bo, b_prev, b_self):
        import jax, jax.numpy as jnp
        import numpy as np
        B, L1, L2, DIN, DOUT, H = (8, 512, 512, 512, 512, 16)
        DH = DOUT // H
        SCALE = 1.0 / np.sqrt(DH).astype(np.float32)
        b, l1, _ = seq1.shape
        l2 = seq2.shape[1]
        query = seq2 + b_self
        key = jnp.concatenate([seq1 + b_prev, seq2 + b_self], 1)
        value = jnp.concatenate([seq1, seq2], 1)
        q = (query @ Wq + bq).reshape(b, l2, H, DH).transpose(0, 2, 1, 3)
        k = (key @ Wk + bk).reshape(b, l1 + l2, H, DH).transpose(0, 2, 1, 3)
        v = (value @ Wv + bv).reshape(b, l1 + l2, H, DH).transpose(0, 2, 1, 3)
        score_prev = jnp.einsum('bhqd,bhkd->bhqk', q, k[:, :, :l1]) * SCALE
        score_self = (q * k[:, :, l1:]).sum(-1, keepdims=True) * SCALE
        mask = jnp.arange(l1)[None, :] < seq_len1[:, None]
        score_prev = jnp.where(mask[:, None, None, :], score_prev, -jnp.inf)
        score = jnp.concatenate([score_prev, score_self], -1)
        weights = jax.nn.softmax(score, axis=-1)
        attn = jnp.einsum('bhqk,bhkd->bhqd', weights[..., :-1], v[:, :, :l1])
        attn = attn + weights[..., -1:] * v[:, :, l1:]
        attn = attn.transpose(0, 2, 1, 3).reshape(b, l2, H * DH)
        return attn @ Wo + bo

    def _L1_cond_ref(x, indices, W1, b1, W2, b2, We, be):
        import jax, jax.numpy as jnp
        import numpy as np
        IN, HID, OUT, PART, E = (512, 2048, 512, 128, 8)
        B, N = (16, 1024)
        h = jax.nn.gelu(jnp.einsum('bni,ih->bnh', x, W1) + b1, approximate=False)
        shared_x = jnp.einsum('bnh,ho->bno', h, W2) + b2
        We_sel = We[indices]
        be_sel = be[indices]
        expert_x = jnp.einsum('bnh,bhp->bnp', h, We_sel) + be_sel[:, None, :]
        return jnp.concatenate([shared_x, expert_x], axis=-1)
    x = x + _L0_cond_ref(x, fside_BxSxS_0, itok_B_18_1004, L0_cond_Wq, L0_cond_bq, L0_cond_Wk, L0_cond_bk, L0_cond_Wv, L0_cond_bv, L0_cond_Wo, L0_cond_bo, L0_cond_b_prev, L0_cond_b_self)
    x = x + _L1_cond_ref(x, itok_B_0_7, L1_cond_W1, L1_cond_b1, L1_cond_W2, L1_cond_b2, L1_cond_We, L1_cond_be)
    return x

_drawn_inputs = setup_inputs


def setup_inputs(seed=0):
    import zlib

    import numpy as np

    out = dict(_drawn_inputs(seed))
    spreads = {'L0_cond_bq': (0.0, 0.8),
     'L0_cond_bk': (0.0, 2.0),
     'L0_cond_bv': (0.0, 0.705),
     'L0_cond_bo': (0.0, 0.306)}
    factors = {'fside_BxSxS_0': 8.0,
     'L0_cond_Wq': 8.0,
     'L0_cond_Wk': 8.0,
     'L0_cond_Wv': 3.721,
     'L0_cond_b_prev': 8.0,
     'L0_cond_b_self': 8.0,
     'L1_cond_b1': 21.333,
     'L1_cond_b2': 18.722,
     'L1_cond_be': 36.132}
    for name, (base, spread) in spreads.items():
        noise = np.random.default_rng([zlib.crc32(name.encode()), seed]).standard_normal(out[name].shape)
        drawn = base * np.exp(spread * noise) if base else spread * noise
        out[name] = jnp.asarray(drawn.astype(out[name].dtype))
    for name, factor in factors.items():
        out[name] = (out[name] * factor).astype(out[name].dtype)
    return out
```

```python
import concourse.bass as bass
from concourse import mybir
from contextlib import ExitStack

F32 = mybir.dt.float32
F32R = mybir.dt.float32r
I32 = mybir.dt.int32
ALU = mybir.AluOpType
ACT = mybir.ActivationFunctionType
AX = mybir.AxisListType


MASKED = -(2.0 ** 100)
DMA = 16


def cond_resid_program(nc, x, seq2, prev_len, expert, Wq, bq, Wk, bk, Wv, bv, Wo, bo, b_prev, b_self,
                       W1, b1, W2, b2, We, be, out):
    B, S, D = x.shape
    P = 128
    C = D // P
    DH = 32
    HG = P // DH
    H = D // DH
    HID = W1.shape[1]
    KH = HID // P
    CS = W2.shape[1] // P
    SCALE = float(DH) ** -0.5
    TILES = HG * C
    LAG = 3
    KM = 3 * DH + 1
    KS = KM + 2
    KE = DH + HG
    QUAD = 32
    assert (S, D, C, HG, H, KH, CS) == (512, 512, 4, 4, 16, 16, 3) and We.shape[2] == P

    attn_dram = nc.dram_tensor("attn_scratch", (B, C, P, S), F32, kind="Internal").ap()
    mask_dram = nc.dram_tensor("mask_scratch", (B, S), F32, kind="Internal").ap()

    keep = ExitStack()

    def sem(name):
        return keep.enter_context(nc.semaphore(name))

    def wait(eng, s, n):
        if not isinstance(n, int) or n > 0:
            eng.wait_ge(s, n)

    def f(ap):
        return ap.bitcast(F32)

    with keep:
        ps_score = [keep.enter_context(nc.psum_tensor(f"ps_score{i}", [P, 512], F32)) for i in range(2)]
        ps_max = [keep.enter_context(nc.psum_tensor(f"ps_max{i}", [P, 512], F32)) for i in range(2)]
        ps_av = [keep.enter_context(nc.psum_tensor(f"ps_av{i}", [P, 512], F32)) for i in range(2)]
        ps_proj = [keep.enter_context(nc.psum_tensor(f"ps_proj{i}", [P, 512], F32)) for i in range(2)]

        one = ExitStack()

        def sb1(name, shape, dt=F32):
            return one.enter_context(nc.sbuf_tensor(name, shape, dt))

        w_hi = sb1("w_hi", [P, 3, C, D], F32R)
        w_lo = sb1("w_lo", [P, 3, C, D], F32R)
        in_hi = sb1("in_hi", [P, 2, C, S], F32R)
        in_lo = sb1("in_lo", [P, 2, C, S], F32R)
        raw = sb1("raw", [P, 4, S])
        turned = sb1("turned", [P, 2, S])
        q_f = sb1("q_f", [P, S])
        parts = sb1("parts", [P, 4, S], F32R)
        k_lo, k_hi, q_hi, q_lo = (parts[:, n, :] for n in range(4))
        qk_f = sb1("qk_f", [P, S])
        qk_hi = sb1("qk_hi", [P, S], F32R)
        qk_lo = sb1("qk_lo", [P, S], F32R)
        v2 = sb1("v2", [P, 4, S])
        num = sb1("num", [P, 2, S])
        den = sb1("den", [P, 2, S])
        m_col = sb1("m_col", [P, C, HG])
        m_row = sb1("m_row", [HG, S])
        m_neg = sb1("m_neg", [KE, S], F32R)
        ident = sb1("ident", [P, P])
        sum_heads = sb1("sum_heads", [P, HG], F32R)
        sum_spread = sb1("sum_spread", [P, P], F32R)
        spread = sb1("spread", [KE, P], F32R)
        bias = sb1("bias", [P, 3, C])
        b_in = sb1("b_in", [P, C, 2])
        b_qk = sb1("b_qk", [P, 2, C])
        before = one.enter_context(ExitStack())
        w_raw = before.enter_context(nc.sbuf_tensor("w_raw", [P, 3, C, D], F32))
        spread_f = before.enter_context(nc.sbuf_tensor("spread_f", [KE, P], F32))
        len_i = before.enter_context(nc.sbuf_tensor("len_i", [B, 1], I32))
        len_f = before.enter_context(nc.sbuf_tensor("len_f", [B, 1], F32))
        pos_i = before.enter_context(nc.sbuf_tensor("pos_i", [B, S], I32))
        pos_f = before.enter_context(nc.sbuf_tensor("pos_f", [B, S], F32))
        mask = before.enter_context(nc.sbuf_tensor("mask", [B, S], F32))
        before.close()
        stacks = sb1("stacks", [P, 2, HG, 2, S], F32R)
        k_st, q_st = stacks[:, :, :, 0], stacks[:, :, :, 1]
        p_f = sb1("p_f", [P, 2, S])
        p_hi = sb1("p_hi", [P, 4, S], F32R)
        p_lo = sb1("p_lo", [P, 4, S], F32R)
        v_st = sb1("v_st", [P, C, H, 3 * DH], F32R)
        one.close()

        two = ExitStack()

        def sb2(name, shape, dt=F32):
            return two.enter_context(nc.sbuf_tensor(name, shape, dt))

        w1_hi = sb2("w1_hi", [P, C, HID], F32R)
        w1_lo = sb2("w1_lo", [P, C, HID], F32R)
        wo_hi = sb2("wo_hi", [P, C, D], F32R)
        wo_lo = sb2("wo_lo", [P, C, D], F32R)
        w2_hi = sb2("w2_hi", [P, KH, CS * P], F32R)
        w2_lo = sb2("w2_lo", [P, KH, CS * P], F32R)
        we_hi = sb2("we_hi", [P, KH, P], F32R)
        we_lo = sb2("we_lo", [P, KH, P], F32R)
        bias_o = sb2("bias_o", [P, C])
        bias_1 = sb2("bias_1", [P, KH])
        bias_2 = sb2("bias_2", [P, C])
        bv_col = sb2("bv_col", [P, C])
        bo_col = sb2("bo_col", [P, C])
        ids = sb2("ids", [1, B], I32)
        we_raw = sb2("we_raw", [P, 4, P])
        a_raw = sb2("a_raw", [P, 2, S])
        a_hi = sb2("a_hi", [P, C, S], F32R)
        a_lo = sb2("a_lo", [P, C, S], F32R)
        x_raw = sb2("x_raw", [P, S])
        x_t = sb2("x_t", [P, S])
        staged = two.enter_context(ExitStack())
        wide = [staged.enter_context(nc.sbuf_tensor(f"wide{i}", [P, 2048], F32)) for i in range(2)]
        staged.close()
        y_f = sb2("y_f", [P, S])
        y_hi = sb2("y_hi", [P, C, S], F32R)
        y_lo = sb2("y_lo", [P, C, S], F32R)
        h_f = sb2("h_f", [P, S])
        h_hi = sb2("h_hi", [P, 2, S], F32R)
        h_lo = sb2("h_lo", [P, 2, S], F32R)
        z_f = sb2("z_f", [P, S])
        z_t = sb2("z_t", [P, 2, S])
        two.close()

        in_landed = [sem(f"in_landed{i}") for i in range(4)]
        w_landed = [sem(f"w_landed{i}") for i in range(3)]
        bias_landed = sem("bias_landed")
        len_landed = sem("len_landed")
        mask_made = sem("mask_made")
        mask_landed = sem("mask_landed")
        consts_made = sem("consts_made")
        w_hi_made = sem("w_hi_made")
        w_lo_made = sem("w_lo_made")
        bias_mm = sem("bias_mm")
        bias_made = sem("bias_made")
        zeros_made = sem("zeros_made")
        ones_made = sem("ones_made")
        turn_made = sem("turn_made")
        in_hi_made = sem("in_hi_made")
        x_lo_made, seq2_lo_made = sem("x_lo_made"), sem("seq2_lo_made")
        q_mm, k_mm, v2_mm, k2_mm = sem("q_mm"), sem("k_mm"), sem("v2_mm"), sem("k2_mm")
        v_mm = sem("v_mm")
        q_f_made, q_hi_made, q_lo_made = sem("q_f_made"), sem("q_hi_made"), sem("q_lo_made")
        k_hi_made, k_lo_made = sem("k_hi_made"), sem("k_lo_made")
        v2_made = sem("v2_made")
        qk_f_made, qk_hi_made, qk_lo_made = sem("qk_f_made"), sem("qk_hi_made"), sem("qk_lo_made")
        v_hi_made, v_lo_made = sem("v_hi_made"), sem("v_lo_made")
        stacked = [[sem(f"stacked{r}_{j}") for j in range(HG)] for r in range(2)]
        max_mm, max_made = sem("max_mm"), sem("max_made")
        own_mm, own_made = sem("own_mm"), sem("own_made")
        turn_mm = sem("turn_mm")
        m_row_made, m_hi_made, m_lo_made = sem("m_row_made"), sem("m_hi_made"), sem("m_lo_made")
        m_landed = [sem(f"m_landed{r}") for r in range(2)]
        ow_mm, ow_made = sem("ow_mm"), sem("ow_made")
        score_mm = sem("score_mm")
        p_f_made, p_hi_made, p_lo_made = sem("p_f_made"), sem("p_hi_made"), sem("p_lo_made")
        av_mm = sem("av_mm")
        av_lo_made = sem("av_lo_made")
        ov_made = sem("ov_made")
        den_made, num_made = sem("den_made"), sem("num_made")
        joined, rden_made = sem("joined"), sem("rden_made")
        attn_made = sem("attn_made")
        attn_stored = [sem(f"attn_stored{r}") for r in range(2)]

        wide_landed = [sem(f"wide_landed{i}") for i in range(2)]
        wide_hi_made, wide_lo_made = sem("wide_hi_made"), sem("wide_lo_made")
        small_landed = sem("small_landed")
        ids_landed = sem("ids_landed")
        bo_mm, bo_made = sem("bo_mm"), sem("bo_made")
        be_landed = sem("be_landed")
        we_landed, we_hi_made, we_lo_made = sem("we_landed"), sem("we_hi_made"), sem("we_lo_made")
        a_landed = [sem(f"a_landed{i}") for i in range(2)]
        a_hi_made, a_lo_made = sem("a_hi_made"), sem("a_lo_made")
        x_landed, x_made = sem("x_landed"), sem("x_made")
        o_mm = sem("o_mm")
        y_f_made, y_hi_made, y_lo_made = sem("y_f_made"), sem("y_hi_made"), sem("y_lo_made")
        h_mm = sem("h_mm")
        h_f_made, h_hi_made, h_lo_made = sem("h_f_made"), sem("h_hi_made"), sem("h_lo_made")
        out_mm = sem("out_mm")
        z_a_made, z_made, z_t_made = sem("z_a_made"), sem("z_made"), sem("z_t_made")
        stored = [sem(f"stored{r}") for r in range(2)]

        block = keep.enter_context(nc.Block())

        def after(b, g, k):
            return b + (g + k) // C, (g + k) % C

        def stack_count(b, c):
            return DMA * (3 * (2 * b + c // 2 + 1) + b + 1)

        def tiles_of_max(i):
            ends = (2, 3, 5, 6, 8, 10, 12, 14, 14, TILES)
            return range(ends[i - 1] if i else 0, ends[i]) if i < len(ends) else range(0)

        turn_at = {(1, 10): (0,), (1, 11): (1,), (1, 12): (2,), (1, 13): (3,), (1, 14): (4,), (1, 15): (5,),
                   (2, 0): (6,), (2, 1): (7,)}
        hi_at = {(1, 11): (0,), (1, 12): (1,), (1, 13): (2,), (1, 14): (3,), (2, 0): (4, 5), (2, 1): (6,), (2, 2): (7,)}
        x_lo_at = {(1, 11): (0,), (1, 12): (1,), (1, 13): (2,), (1, 14): (3,)}
        seq2_lo_at = {(2, 0): (4,), (2, 1): (5,), (2, 2): (6,), (2, 3): (7,)}

        def blocks(t, b, c, q):
            return t[bass.ds(b, 1)].rearrange("o (tb ti) f -> (o ti) tb f", ti=QUAD)[
                :, :, c * P + QUAD * q:c * P + QUAD * (q + 1)]

        def batches(eng, run):
            run(0, True, False)
            with eng.Fori(1, B - 1) as b:
                run(b, False, False)
            run(B - 1, False, True)

        ps_out = ps_score + ps_max

        wide_pieces = [(Wo, slice(0, C))]
        wide_pieces += [(W1, slice(k, k + 1)) for k in range(C)]
        wide_pieces += [(W2, slice(k, k + 4)) for k in range(0, KH, 4)]

        def wide_view(n):
            src, at = wide_pieces[n]
            k, cols = at.stop - at.start, src.shape[1]
            return wide[n % 2][:, 0:k * cols].rearrange("p (k n) -> p k n", k=k)

        def wide_parts(n):
            src, at = wide_pieces[n]
            hi, lo = {0: (wo_hi, wo_lo)}.get(n, (w1_hi, w1_lo) if n <= C else (w2_hi, w2_lo))
            return hi[:, at], lo[:, at]

        @block.sync
        def _(sp):
            def column(dst, src):
                sp.dma_start(dst, src.rearrange("(c p) -> p c", p=P), allow_slow_non_contiguous=True).then_inc(bias_landed, DMA)

            for n, w in enumerate((Wq, Wk, Wv)):
                sp.dma_start(w_raw[:, n], w.rearrange("(c p) n -> p c n", p=P)).then_inc(w_landed[n], DMA)
            sp.dma_start(len_i[:, :], prev_len.rearrange("(b o) -> b o", o=1)).then_inc(len_landed, DMA)
            column(b_in[:, :, 0], b_prev.rearrange("a o d -> (a o d)"))
            column(b_in[:, :, 1], b_self.rearrange("a o d -> (a o d)"))
            column(b_qk[:, 0, :], bq)
            column(b_qk[:, 1, :], bk)

            def load(b, j):
                k = 8 * b + j
                src = x if j < C else seq2
                wait(sp, turn_made, k - 3)
                for q in range(P // QUAD):
                    sp.dma_start(raw[QUAD * q:QUAD * (q + 1), j % 4].rearrange("p (tb f) -> p tb f", f=QUAD),
                                 blocks(src, b, j % C, q)).then_inc(in_landed[j % 4], DMA)

            def stack(b, c, j):
                G, r = C * b + c, c % 2
                if j == 0:
                    wait(sp, q_lo_made, G + 1)
                    wait(sp, k_lo_made, G + 1)
                wait(sp, score_mm, TILES * (G - 2) + C * (j + 1))
                if c < 2:
                    sp.dma_start(f(k_st[KM - 1:KM, r, j]), mask_dram[bass.ds(b, 1)]).then_inc(stacked[r][j], DMA)
                rows = slice(DH * j, DH * (j + 1))
                for n, pair in enumerate((parts[rows, 1:3], parts[rows, 0:3:2], parts[rows, 1:4:2])):
                    sp.dma_start(f(stacks[DH * n:DH * (n + 1), r, j]), f(pair)).then_inc(stacked[r][j], DMA)

            def store(b, c):
                wait(sp, attn_made, C * b + c + 1)
                sp.dma_start(attn_dram[bass.ds(b, 1), c].rearrange("o p s -> (o p) s"),
                             num[:, c % 2]).then_inc(attn_stored[c % 2], DMA)

            for j in range(2 * C):
                load(0, j)
            sp.wait_ge(mask_made, 1)
            sp.dma_start(mask_dram, mask[:, :]).then_inc(mask_landed, DMA)
            sp.wait_ge(mask_landed, DMA)
            sp.wait_ge(ones_made, 1)
            for c in range(2):
                for j in range(HG):
                    stack(0, c, j)

            def batch(b, first, last):
                for g in range(C):
                    more = not (last and g >= 2)
                    if g == 1 and not last:
                        for j in range(C):
                            load(b + 1, j)
                    if more:
                        for j in range(HG):
                            if g == 1 and j == HG - 1 and not last:
                                for t in range(C, 2 * C):
                                    load(b + 1, t)
                            stack(*after(b, g, 2), j)
                    if not (first and g == 0):
                        store(*after(b, g, -1))

            batches(sp, batch)
            store(B - 1, C - 1)

            for r in range(2):
                sp.wait_ge(attn_stored[r], DMA * C * B // 2)
            sp.dma_start(ids[:, :], expert.rearrange("(o b) -> o b", o=1)).then_inc(ids_landed, DMA)
            for dst, src in ((bv_col[:, :], bv), (bo_col[:, :], bo), (bias_1[:, :], b1), (bias_2[:, 0:CS], b2)):
                sp.dma_start(dst, src.rearrange("(c p) -> p c", p=P), allow_slow_non_contiguous=True).then_inc(small_landed, DMA)

            def weights(n):
                src, at = wide_pieces[n]
                wait(sp, wide_lo_made, n - 1)
                if n == 2:
                    sp.wait_ge(bo_mm, 1)
                sp.dma_start(wide_view(n), src.rearrange("(k p) n -> p k n", p=P)[:, at]).then_inc(wide_landed[n % 2], DMA)

            def expert_weights(b, j):
                e = sp.value_load(ids[0:1, bass.ds(b, 1)], min_val=0, max_val=We.shape[0] - 1)
                src = We[bass.ds(e, 1)].rearrange("o (k p) n -> p (o k) n", p=P)[:, 4 * j:4 * j + 4]
                wait(sp, we_lo_made, 4 * b + j)
                sp.dma_start(we_raw[:, :, :], src).then_inc(we_landed, DMA)

            def expert_bias(b):
                e = sp.value_load(ids[0:1, bass.ds(b, 1)], min_val=0, max_val=be.shape[0] - 1)
                wait(sp, z_a_made, C * b)
                sp.dma_start(bias_2[:, CS:C], be[bass.ds(e, 1)].rearrange("o p -> p o"), allow_slow_non_contiguous=True).then_inc(be_landed, DMA)

            def attended(b, c):
                wait(sp, a_lo_made, C * b + c - 1)
                sp.dma_start(a_raw[:, c % 2], attn_dram[bass.ds(b, 1), c].rearrange("o p s -> (o p) s")).then_inc(a_landed[c % 2], DMA)

            def residual(b, c):
                wait(sp, x_made, C * b + c)
                for q in range(P // QUAD):
                    sp.dma_start(x_raw[QUAD * q:QUAD * (q + 1), :].rearrange("p (tb f) -> p tb f", f=QUAD),
                                 blocks(x, b, c, q)).then_inc(x_landed, DMA)

            def result(b, c):
                dve_count = C * b + c + 1
                sp.wait_ge(z_t_made, dve_count)
                for q in range(P // QUAD):
                    sp.dma_start(blocks(out, b, c, q),
                                 z_t[QUAD * q:QUAD * (q + 1), c % 2].rearrange("p (tb f) -> p tb f", f=QUAD)
                                 ).then_inc(stored[c % 2], DMA)

            sp.wait_ge(ids_landed, DMA)
            weights(0)
            weights(1)
            for c in range(C):
                if c < 2:
                    attended(0, c)
            residual(0, 0)
            expert_bias(0)
            expert_weights(0, 0)
            for n in range(2, len(wide_pieces)):
                weights(n)
            for c in range(2, C):
                attended(0, c)
            expert_weights(0, 1)
            expert_weights(0, 2)
            for c in range(1, C):
                residual(0, c)

            def rows(b, first, last):
                expert_weights(b, 3)
                if not last:
                    expert_weights(b + 1, 0)
                    for c in range(C):
                        attended(b + 1, c)
                    expert_weights(b + 1, 1)
                    expert_weights(b + 1, 2)
                for c in range(C):
                    if not last:
                        residual(b + 1, c)
                    result(b, c)
                if not last:
                    expert_bias(b + 1)

            batches(sp, rows)
            for r in range(2):
                sp.wait_ge(stored[r], (P // QUAD) * DMA * C * B // 2)

        @block.gpsimd
        def _(pool):
            pool.memset(ident[:, :], 0.0).then_inc(consts_made, 1)
            pool.memset(spread_f[:, :], 0.0).then_inc(consts_made, 1)
            pool.iota(pos_i[:, :], pattern=[[1, S]], base=0, channel_multiplier=0).then_inc(consts_made, 1)
            pool.wait_ge(consts_made, 2)
            pool.affine_select(out=ident[:, :], in_=ident[:, :], compare_op=ALU.not_equal, fill=1.0, base=0,
                               pattern=[[-1, P]], channel_multiplier=1).then_inc(consts_made, 1)
            for n in range(2):
                pool.wait_ge(consts_made, 4 + n)
                pool.affine_select(out=spread_f[:, :].rearrange("k (j d) -> k j d", d=DH),
                                   in_=spread_f[:, :].rearrange("k (j d) -> k j d", d=DH),
                                   compare_op=ALU.not_equal, fill=1.0, base=-QUAD * n,
                                   pattern=[[-1, HG], [0, DH]], channel_multiplier=1).then_inc(consts_made, 1)

            def p_low(b, g, i):
                T = TILES * (C * b + g) + i
                pool.wait_ge(p_hi_made, T + 1)
                pool.tensor_tensor(p_lo[:, i % 4], p_f[:, i % 2], f(p_hi[:, i % 4]),
                                   ALU.subtract).then_inc(p_lo_made, 1)

            def own_value(b, c):
                G = C * b + c
                pool.wait_ge(ow_made, G + 1)
                pool.wait_ge(v2_made, G + 1)
                pool.tensor_tensor(v2[:, c], v2[:, c], den[:, c % 2], ALU.mult).then_inc(ov_made, 1)

            def add_own(b, c):
                G, r = C * b + c, c % 2
                pool.wait_ge(num_made, HG * (G + 1))
                pool.wait_ge(ov_made, G + 1)
                pool.tensor_tensor(num[:, r], num[:, r], v2[:, c], ALU.add).then_inc(joined, 1)

            def x_low(b, j):
                pool.wait_ge(in_hi_made, 2 * C * b + j + 1)
                pool.tensor_tensor(in_lo[:, 1, j], turned[:, j % 2], f(in_hi[:, 1, j]),
                                   ALU.subtract).then_inc(x_lo_made, 1)

            for j in range(C):
                x_low(0, j)

            def batch(b, first, last):
                for g in range(C):
                    for i in range(TILES):
                        p_low(b, g, i)
                        if not last:
                            for j in x_lo_at.get((g, i), ()):
                                x_low(b + 1, j)
                        if i == 4:
                            own_value(b, g)
                        if i == 7 and not (first and g == 0):
                            add_own(*after(b, g, -1))

            batches(pool, batch)
            add_own(B - 1, C - 1)

        @block.scalar
        def _(act):
            for n in range(3):
                act.wait_ge(w_landed[n], DMA)
                for c in range(C):
                    act.copy(w_hi[:, n, c], w_raw[:, n, c]).then_inc(w_hi_made, 1)

            def in_high(b, j):
                k = 2 * C * b + j
                act.wait_ge(turn_made, k + 1)
                wait(act, k_mm if j < C else k2_mm, C * b)
                act.copy(in_hi[:, 1 - j // C, j % C], turned[:, j % 2]).then_inc(in_hi_made, 1)

            def q_out(b, c):
                G = C * b + c
                act.wait_ge(q_mm, G + 1)
                wait(act, qk_f_made, G)
                act.activation(q_f[:, :], ps_proj[0][:, :], ACT.Identity,
                               bias=bias[:, 0, c:c + 1]).then_inc(q_f_made, 1)
                pb, pc = after(b, c, -1)
                for j in range(HG):
                    wait(act, stacked[pc % 2][j], stack_count(pb, pc))
                act.activation(q_hi[:, :], ps_proj[0][:, :], ACT.Identity,
                               bias=bias[:, 0, c:c + 1]).then_inc(q_hi_made, 1)

            def k_out(b, c):
                act.wait_ge(k_mm, C * b + c + 1)
                act.activation(k_hi[:, :], ps_proj[1][:, :], ACT.Identity,
                               bias=bias[:, 1, c:c + 1]).then_inc(k_hi_made, 1)

            def v2_out(b, c):
                G = C * b + c
                act.wait_ge(v2_mm, G + 1)
                wait(act, attn_made, G - 3)
                act.copy(v2[:, c], ps_proj[0][:, :]).then_inc(v2_made, 1)

            def qk_high(b, c):
                G = C * b + c
                act.wait_ge(qk_f_made, G + 1)
                wait(act, ow_mm, G)
                act.copy(qk_hi[:, :], qk_f[:, :]).then_inc(qk_hi_made, 1)

            def v_high(b, t):
                act.wait_ge(v_mm, C * b + t + 1)
                wait(act, av_mm, C * TILES * b)
                act.copy(v_st[:, t, :, 0:DH],
                         ps_proj[t % 2][:, :].rearrange("p (h d) -> p h d", d=DH)).then_inc(v_hi_made, 1)

            def own_row(b, c):
                G = C * b + c
                act.wait_ge(own_mm, G + 1)
                wait(act, m_lo_made, G)
                act.copy(m_row[:, :], ps_max[1][0:HG, :]).then_inc(own_made, 1)

            def m_high(b, c):
                G = C * b + c
                act.wait_ge(m_row_made, G + 1)
                pb, pc = after(b, c, -1)
                wait(act, m_landed[pc % 2], 2 * DMA * (2 * pb + pc // 2 + 1))
                wait(act, ow_mm, G)
                act.mul(m_neg[0:HG, :], m_row[:, :], -1.0).then_inc(m_hi_made, 1)

            def maxima(b, c):
                G, r = C * b + c, c % 2
                wait(act, m_lo_made, G + 1)
                for n in range(2):
                    act.dma_start(f(q_st[KM + n:KM + n + 1, r]),
                                  f(m_neg[QUAD * n:QUAD * n + HG])).then_inc(m_landed[r], DMA)

            def own_weight(b, c):
                G = C * b + c
                act.wait_ge(ow_mm, G + 1)
                wait(act, attn_made, G - 1)
                act.activation(den[:, c % 2], ps_max[1][:, :], ACT.Exp, scale=SCALE).then_inc(ow_made, 1)

            def probabilities(b, g, i):
                T = TILES * (C * b + g) + i
                act.wait_ge(score_mm, T + 1)
                wait(act, p_lo_made, T - 1)
                act.activation(p_f[:, i % 2], ps_score[i % 2][:, :], ACT.Exp, scale=SCALE).then_inc(p_f_made, 1)
                wait(act, av_mm, T - 3)
                act.activation(p_hi[:, i % 4], ps_score[i % 2][:, :], ACT.Exp, scale=SCALE).then_inc(p_hi_made, 1)

            def av_low(b, g, j):
                Hd = HG * (C * b + g) + j
                act.wait_ge(av_mm, C * (Hd + 1))
                if j == 0:
                    wait(act, attn_stored[g % 2], DMA * (2 * b + g // 2))
                act.copy(num[DH * j:DH * (j + 1), g % 2], ps_av[j % 2][DH:2 * DH, :]).then_inc(av_lo_made, 1)

            for j in range(2 * C):
                in_high(0, j)
            act.wait_ge(bias_made, 1)
            q_out(0, 0)
            k_out(0, 0)
            v2_out(0, 0)
            qk_high(0, 0)
            q_out(0, 1)
            k_out(0, 1)
            v2_out(0, 1)
            own_row(0, 0)
            m_high(0, 0)
            maxima(0, 0)
            own_weight(0, 0)

            def batch(b, first, last):
                for g in range(C):
                    nxt, nxt2 = after(b, g, 1), after(b, g, 2)
                    project = not (last and g >= 2)
                    maximum = not (last and g == C - 1)
                    for i in range(TILES):
                        probabilities(b, g, i)
                        if i == 0 and not (first and g == 0):
                            av_low(*after(b, g, -1), HG - 2)
                        if i == 1 and maximum:
                            qk_high(*nxt)
                        if i == 3 and not (first and g == 0):
                            av_low(*after(b, g, -1), HG - 1)
                        if g == 0 and 2 <= i < 2 + C:
                            v_high(b, i - 2)
                        if not last:
                            for j in hi_at.get((g, i), ()):
                                in_high(b + 1, j)
                        if i == 7 and project:
                            q_out(*nxt2)
                        if i == 8:
                            av_low(b, g, 0)
                        if i == 10 and project:
                            k_out(*nxt2)
                        if i == 11 and maximum:
                            own_row(*nxt)
                        if i == 12 and maximum:
                            m_high(*nxt)
                        if i == 12:
                            av_low(b, g, 1)
                        if i == 13 and maximum:
                            maxima(*nxt)
                        if i == 13 and project:
                            v2_out(*nxt2)
                        if i == 15 and maximum:
                            own_weight(*nxt)

            batches(act, batch)
            av_low(B - 1, C - 1, HG - 2)
            av_low(B - 1, C - 1, HG - 1)

            for n in range(len(wide_pieces)):
                act.wait_ge(wide_landed[n % 2], DMA * (n // 2 + 1))
                act.copy(wide_parts(n)[0], wide_view(n)).then_inc(wide_hi_made, 1)

            def expert_high(b, j):
                act.wait_ge(we_landed, DMA * (4 * b + j + 1))
                wait(act, out_mm, KH * (b - 1) + 4 * j + 4)
                act.copy(we_hi[:, 4 * j:4 * j + 4], we_raw[:, :, :]).then_inc(we_hi_made, 1)

            def attended_high(b, c):
                act.wait_ge(a_landed[c % 2], DMA * (2 * b + c // 2 + 1))
                wait(act, o_mm, C * b)
                act.copy(a_hi[:, c], a_raw[:, c % 2]).then_inc(a_hi_made, 1)

            def y_high(b, c):
                act.wait_ge(y_f_made, C * b + c + 1)
                wait(act, h_mm, KH * b)
                wait(act, z_made, C * (b - 1) + c + 1)
                act.copy(y_hi[:, c], y_f[:, :]).then_inc(y_hi_made, 1)

            def hidden(b, m):
                n = KH * b + m
                act.wait_ge(h_mm, n + 1)
                wait(act, h_lo_made, n)
                act.activation(h_f[:, :], ps_av[m % 2][:, :], ACT.Gelu, bias=bias_1[:, m:m + 1]).then_inc(h_f_made, 1)
                wait(act, out_mm, n - 1)
                act.activation(h_hi[:, m % 2], ps_av[m % 2][:, :], ACT.Gelu, bias=bias_1[:, m:m + 1]).then_inc(h_hi_made, 1)

            act.wait_ge(small_landed, 4 * DMA)
            expert_high(0, 0)
            for c in range(C):
                attended_high(0, c)
            expert_high(0, 1)
            expert_high(0, 2)
            for c in range(C):
                y_high(0, c)

            def rows(b, first, last):
                for m in range(KH):
                    hidden(b, m)
                    if m == 2:
                        expert_high(b, 3)
                    if not last and m in (6, 10, 14):
                        expert_high(b + 1, m // 4 - 1)
                    if not last and 7 <= m < 7 + C:
                        attended_high(b + 1, m - 7)
                if not last:
                    for c in range(C):
                        y_high(b + 1, c)

            batches(act, rows)

        @block.vector
        def _(dve):
            dve.memset(f(sum_heads[:, :]), 0.0).then_inc(zeros_made, 1)
            dve.memset(f(sum_spread[:, :]), 0.0).then_inc(zeros_made, 1)
            dve.memset(f(m_neg[:, :]), 0.0).then_inc(zeros_made, 1)
            dve.wait_ge(zeros_made, 3)
            for j in range(HG):
                rows = slice(DH * j, DH * (j + 1))
                dve.memset(f(sum_heads[rows, j:j + 1]), 1.0).then_inc(zeros_made, 1)
                dve.memset(f(sum_spread[rows, rows]), 1.0).then_inc(zeros_made, 1)
            dve.wait_ge(consts_made, 6)
            dve.tensor_copy(spread[:, :], spread_f[:, :]).then_inc(zeros_made, 1)

            dve.wait_ge(len_landed, DMA)
            dve.tensor_copy(len_f[:, :], len_i[:, :]).then_inc(zeros_made, 1)
            dve.tensor_copy(pos_f[:, :], pos_i[:, :]).then_inc(zeros_made, 1)
            dve.wait_ge(zeros_made, 3 + 2 * HG + 3)
            dve.tensor_scalar(mask[:, :], pos_f[:, :], len_f[:, 0:1], MASKED, ALU.is_ge, ALU.mult).then_inc(mask_made, 1)

            for n in range(3):
                for c in range(C):
                    dve.wait_ge(w_hi_made, C * n + c + 1)
                    dve.tensor_tensor(w_lo[:, n, c], w_raw[:, n, c], f(w_hi[:, n, c]), ALU.subtract).then_inc(w_lo_made, 1)

            def turn(b, j):
                k = 2 * C * b + j
                dve.wait_ge(in_landed[j % 4], (P // QUAD) * DMA * (2 * b + j // 4 + 1))
                if j < 2:
                    wait(dve, seq2_lo_made, C * (b - 1) + j + 3)
                elif j < C + 2:
                    dve.wait_ge(x_lo_made, C * b + j - 1)
                else:
                    dve.wait_ge(seq2_lo_made, C * b + j - 5)
                dve.transpose(turned[:, j % 2], raw[:, j % 4]).then_inc(turn_made, 1)

            def seq2_low(b, j):
                dve.wait_ge(in_hi_made, 2 * C * b + j + 1)
                dve.tensor_tensor(in_lo[:, 0, j % C], turned[:, j % 2], f(in_hi[:, 0, j % C]),
                                  ALU.subtract).then_inc(seq2_lo_made, 1)

            def q_low(b, c):
                dve.wait_ge(q_hi_made, C * b + c + 1)
                dve.tensor_tensor(q_lo[:, :], q_f[:, :], f(q_hi[:, :]), ALU.subtract).then_inc(q_lo_made, 1)

            def k_low(b, c):
                dve.wait_ge(k_hi_made, C * b + c + 1)
                dve.scalar_tensor_tensor(out=k_lo[:, :], in0=ps_proj[1][:, :], scalar=bias[:, 1, c:c + 1],
                                         in1=f(k_hi[:, :]), op0=ALU.add, op1=ALU.subtract).then_inc(k_lo_made, 1)

            def qk(b, c):
                G = C * b + c
                dve.wait_ge(k2_mm, G + 1)
                dve.wait_ge(q_hi_made, G + 1)
                wait(dve, qk_lo_made, G)
                dve.scalar_tensor_tensor(out=qk_f[:, :], in0=ps_proj[1][:, :], scalar=bias[:, 2, c:c + 1],
                                         in1=q_f[:, :], op0=ALU.add, op1=ALU.mult).then_inc(qk_f_made, 1)

            def qk_low(b, c):
                dve.wait_ge(qk_hi_made, C * b + c + 1)
                dve.tensor_tensor(qk_lo[:, :], qk_f[:, :], f(qk_hi[:, :]), ALU.subtract).then_inc(qk_lo_made, 1)

            def v_low(b, t):
                dve.wait_ge(v_hi_made, C * b + t + 1)
                dve.tensor_tensor(v_st[:, t, :, DH:2 * DH], ps_proj[t % 2][:, :].rearrange("p (h d) -> p h d", d=DH),
                                  f(v_st[:, t, :, 0:DH]), ALU.subtract).then_inc(v_lo_made, 1)

            def maximum(b, c, n):
                G = C * b + c
                dve.wait_ge(max_mm, TILES * G + n + 1)
                if n == 0:
                    wait(dve, turn_mm, G)
                dve.tensor_reduce(m_col[:, n % C, n // C:n // C + 1], ps_max[n % 2][:, :], AX.X,
                                  ALU.max).then_inc(max_made, 1)

            def max_row(b, c):
                G = C * b + c
                dve.wait_ge(own_made, G + 1)
                dve.wait_ge(turn_mm, G + 1)
                dve.tensor_tensor(m_row[:, :], ps_max[0][0:HG, :], m_row[:, :], ALU.max).then_inc(m_row_made, 1)

            def m_low(b, c):
                dve.wait_ge(m_hi_made, C * b + c + 1)
                dve.scalar_tensor_tensor(out=m_neg[QUAD:QUAD + HG, :], in0=m_row[:, :], scalar=-1.0,
                                         in1=f(m_neg[0:HG, :]), op0=ALU.mult, op1=ALU.subtract).then_inc(m_lo_made, 1)

            def head(b, g, j):
                G = C * b + g
                Hd = HG * G + j
                rows = slice(DH * j, DH * (j + 1))
                dve.wait_ge(ov_made, G + 1)
                dve.wait_ge(av_lo_made, Hd + 1)
                dve.tensor_tensor(den[rows, g % 2], ps_av[j % 2][2 * DH:3 * DH, :], den[rows, g % 2],
                                  ALU.add).then_inc(den_made, 1)
                dve.tensor_tensor(num[rows, g % 2], ps_av[j % 2][0:DH, :], num[rows, g % 2],
                                  ALU.add).then_inc(num_made, 1)

            def one_over_den(b, g, n):
                G, r = C * b + g, g % 2
                dve.wait_ge(den_made, HG * (G + 1))
                at = slice(S // 2 * n, S // 2 * (n + 1))
                dve.reciprocal(den[:, r, at], den[:, r, at]).then_inc(rden_made, 1)

            def normalize(b, g):
                G, r = C * b + g, g % 2
                dve.wait_ge(rden_made, 2 * (G + 1))
                dve.wait_ge(joined, G + 1)
                dve.tensor_tensor(num[:, r], num[:, r], den[:, r], ALU.mult).then_inc(attn_made, 1)

            for j in range(2 * C):
                turn(0, j)
                if j >= C:
                    seq2_low(0, j)

            dve.wait_ge(bias_mm, 1)
            dve.wait_ge(bias_landed, 4 * DMA)
            for n, (w, s) in enumerate(((0, 1), (1, 0), (1, 1))):
                col = ps_av[0][:, 0:4 * C].rearrange("p (w c s) -> p w c s", w=2, s=2)[:, w, :, s]
                last = dve.tensor_tensor(bias[:, n, :], col, b_qk[:, w, :], ALU.add)
            last.then_inc(bias_made, 1)

            dve.wait_ge(w_lo_made, 3 * C)
            dve.memset(f(stacks[KM - 1:KS, :, :, :, :]), 1.0).then_inc(zeros_made, 1)
            dve.wait_ge(mask_landed, DMA)
            dve.memset(f(v_st[:, :, :, 2 * DH:3 * DH]), 1.0).then_inc(ones_made, 1)

            q_low(0, 0)
            k_low(0, 0)
            qk(0, 0)
            qk_low(0, 0)
            q_low(0, 1)
            k_low(0, 1)
            for n in range(TILES):
                maximum(0, 0, n)
            max_row(0, 0)
            m_low(0, 0)

            def batch(b, first, last):
                for g in range(C):
                    nxt, nxt2 = after(b, g, 1), after(b, g, 2)
                    project = not (last and g >= 2)
                    bound = not (last and g == C - 1)
                    started = not (first and g == 0)
                    for i in range(TILES):
                        if bound:
                            for n in tiles_of_max(i):
                                maximum(*nxt, n)
                        if g == 0 and 2 <= i < 2 + C:
                            v_low(b, i - 2)
                        if i == 0 and bound:
                            qk(*nxt)
                        if i == 1 and started:
                            head(*after(b, g, -1), HG - 2)
                        if i == 2 and bound:
                            qk_low(*nxt)
                        if i == 3 and started:
                            head(*after(b, g, -1), HG - 1)
                        if not last:
                            for j in seq2_lo_at.get((g, i), ()):
                                seq2_low(b + 1, j)
                            for j in turn_at.get((g, i), ()):
                                turn(b + 1, j)
                        if i == 8 and project:
                            q_low(*nxt2)
                        if i == 8:
                            head(b, g, 0)
                        if i == 10 and project:
                            k_low(*nxt2)
                        if i == 10 and started:
                            one_over_den(*after(b, g, -1), 0)
                        if i == 11 and bound:
                            max_row(*nxt)
                        if i == 12 and bound:
                            m_low(*nxt)
                        if i == 12:
                            head(b, g, 1)
                        if i == 13 and started:
                            one_over_den(*after(b, g, -1), 1)
                        if i == 14 and started:
                            normalize(*after(b, g, -1))

            batches(dve, batch)
            for j in (HG - 2, HG - 1):
                head(B - 1, C - 1, j)
            for n in range(2):
                one_over_den(B - 1, C - 1, n)
            normalize(B - 1, C - 1)

            for n in range(len(wide_pieces)):
                hi, lo = wide_parts(n)
                dve.wait_ge(wide_hi_made, n + 1)
                dve.tensor_tensor(lo, wide_view(n), f(hi), ALU.subtract).then_inc(wide_lo_made, 1)

            dve.wait_ge(bo_mm, 1)
            dve.wait_ge(small_landed, 4 * DMA)
            dve.tensor_tensor(bias_o[:, :], ps_proj[0][:, 0:C], bo_col[:, :], ALU.add).then_inc(bo_made, 1)

            def expert_low(b, j):
                dve.wait_ge(we_hi_made, 4 * b + j + 1)
                dve.tensor_tensor(we_lo[:, 4 * j:4 * j + 4], we_raw[:, :, :], f(we_hi[:, 4 * j:4 * j + 4]),
                                  ALU.subtract).then_inc(we_lo_made, 1)

            def attended_low(b, c):
                dve.wait_ge(a_hi_made, C * b + c + 1)
                dve.tensor_tensor(a_lo[:, c], a_raw[:, c % 2], f(a_hi[:, c]), ALU.subtract).then_inc(a_lo_made, 1)

            def turn_x(b, c):
                n = C * b + c
                dve.wait_ge(x_landed, (P // QUAD) * DMA * (n + 1))
                wait(dve, y_f_made, n)
                dve.transpose(x_t[:, :], x_raw[:, :]).then_inc(x_made, 1)

            def y_out(b, c):
                n = C * b + c
                dve.wait_ge(o_mm, n + 1)
                dve.wait_ge(x_made, n + 1)
                wait(dve, y_lo_made, n)
                dve.scalar_tensor_tensor(out=y_f[:, :], in0=ps_proj[c % 2][:, :], scalar=bias_o[:, c:c + 1],
                                         in1=x_t[:, :], op0=ALU.add, op1=ALU.add).then_inc(y_f_made, 1)

            def y_low(b, c):
                dve.wait_ge(y_hi_made, C * b + c + 1)
                dve.tensor_tensor(y_lo[:, c], y_f[:, :], f(y_hi[:, c]), ALU.subtract).then_inc(y_lo_made, 1)

            def hidden_low(b, m):
                dve.wait_ge(h_hi_made, KH * b + m + 1)
                dve.tensor_tensor(h_lo[:, m % 2], h_f[:, :], f(h_hi[:, m % 2]), ALU.subtract).then_inc(h_lo_made, 1)

            def result(b, c):
                n = C * b + c
                dve.wait_ge(out_mm, KH * (b + 1))
                if c == CS:
                    dve.wait_ge(be_landed, DMA * (b + 1))
                wait(dve, z_t_made, n)
                dve.scalar_tensor_tensor(out=z_f[:, :], in0=ps_out[c][:, :], scalar=bias_2[:, c:c + 1],
                                         in1=f(y_hi[:, c]), op0=ALU.add, op1=ALU.add).then_inc(z_a_made, 1)
                dve.wait_ge(z_a_made, n + 1)
                dve.tensor_tensor(z_f[:, :], z_f[:, :], f(y_lo[:, c]), ALU.add).then_inc(z_made, 1)
                dve.wait_ge(z_made, n + 1)
                wait(dve, stored[c % 2], (P // QUAD) * DMA * (2 * b + c // 2))
                dve.transpose(z_t[:, c % 2], z_f[:, :]).then_inc(z_t_made, 1)

            dve.wait_ge(wide_lo_made, len(wide_pieces))
            dve.wait_ge(bo_made, 1)
            expert_low(0, 0)
            for c in range(C):
                attended_low(0, c)
            expert_low(0, 1)
            expert_low(0, 2)
            for c in range(C):
                turn_x(0, c)
                y_out(0, c)
                y_low(0, c)

            def rows(b, first, last):
                for m in range(KH):
                    hidden_low(b, m)
                    if m == 2:
                        expert_low(b, 3)
                    if not last and m in (6, 10, 14):
                        expert_low(b + 1, m // 4 - 1)
                    if not last and 7 <= m < 7 + C:
                        attended_low(b + 1, m - 7)
                    if not last and m == KH - 1:
                        turn_x(b + 1, 0)
                for c in range(C):
                    result(b, c)
                    if not last:
                        if c > 0:
                            turn_x(b + 1, c)
                        y_out(b + 1, c)
                        y_low(b + 1, c)

            batches(dve, rows)

        @block.tensor
        def _(pe):
            def three(ps, left, right, first, last):
                pe.matmul(ps, left[0], right[0], start=first, stop=False)
                pe.matmul(ps, left[0], right[1], start=False, stop=False)
                return pe.matmul(ps, left[1], right[0], start=False, stop=last)

            pe.wait_ge(bias_landed, 4 * DMA)
            for w in range(2):
                pe.wait_ge(w_landed[w], DMA)
                for c in range(C):
                    at = 2 * (C * w + c)
                    for k in range(C):
                        mm = pe.matmul(ps_av[0][:, at:at + 2], w_raw[:, w, k, P * c:P * (c + 1)], b_in[:, k, :],
                                       start=(k == 0), stop=(k == C - 1))
            mm.then_inc(bias_mm, 1)

            def weight(w, k, c):
                at = slice(P * c, P * (c + 1))
                return w_hi[:, w, k, at], w_lo[:, w, k, at]

            def feature(s, k):
                return in_hi[:, s, k], in_lo[:, s, k]

            def project(b, c, n, third):
                G = C * b + c
                ps = ps_proj[n % 2][:, :]
                w, s, done = ((0, 0, q_mm), (1, 1, k_mm), (2, 0, v2_mm), (1, 0, k2_mm))[n]
                if third == 0:
                    if n == 0:
                        pe.wait_ge(seq2_lo_made, C * (b + 1))
                        wait(pe, v2_made, G)
                        if c == 2:
                            pe.wait_ge(v_lo_made, C * b + C - 1)
                    if n == 1:
                        pe.wait_ge(x_lo_made, C * (b + 1))
                        wait(pe, qk_f_made, G)
                        if c == 2:
                            pe.wait_ge(v_lo_made, C * b + C)
                    if n == 2:
                        pe.wait_ge(q_hi_made, G + 1)
                    if n == 3:
                        pe.wait_ge(k_lo_made, G + 1)
                m = 0
                for k in range(C):
                    (l_hi, l_lo), (r_hi, r_lo) = weight(w, k, c), feature(s, k)
                    for left, right in ((l_hi, r_hi), (l_hi, r_lo), (l_lo, r_hi)):
                        if m // C == third:
                            mm = pe.matmul(ps, left, right, start=(m == 0), stop=(m == 3 * C - 1))
                        m += 1
                if third == 2:
                    mm.then_inc(done, 1)

            def values(b, t):
                ps = ps_proj[t % 2][:, :]
                if t == 0:
                    wait(pe, v2_made, C * b + 2)
                if t == 1:
                    wait(pe, qk_f_made, C * b + 2)
                if t >= 2:
                    pe.wait_ge(v_lo_made, C * b + t - 1)
                keys = slice(P * t, P * (t + 1))
                for k in range(C):
                    mm = three(ps, (in_hi[:, 1, k, keys], in_lo[:, 1, k, keys]), (w_hi[:, 2, k], w_lo[:, 2, k]),
                               k == 0, k == C - 1)
                mm.then_inc(v_mm, 1)

            def max_tile(b, c, n):
                G, r, j, t = C * b + c, c % 2, n // C, n % C
                if t == 0:
                    pe.wait_ge(stacked[r][j], stack_count(b, c))
                wait(pe, max_made, TILES * G + n - 1)
                if n == 0:
                    wait(pe, m_row_made, G)
                if n == 1:
                    wait(pe, ow_made, G)
                pe.matmul(ps_max[n % 2][:, :], q_st[0:KM, r, j, P * t:P * (t + 1)], k_st[0:KM, r, j, :],
                          start=True, stop=True).then_inc(max_mm, 1)

            def own_scores(b, c):
                G = C * b + c
                pe.wait_ge(qk_lo_made, G + 1)
                pe.wait_ge(max_made, TILES * (G + 1))
                pe.matmul(ps_max[1][0:HG, :], sum_heads[:, :], qk_hi[:, :], start=True, stop=False)
                pe.matmul(ps_max[1][0:HG, :], sum_heads[:, :], qk_lo[:, :], start=False, stop=True).then_inc(own_mm, 1)

            def turn_max(b, c):
                pe.wait_ge(max_made, TILES * (C * b + c + 1))
                for t in range(C):
                    mm = pe.matmul(ps_max[0][0:HG, P * t:P * (t + 1)], m_col[:, t, :], ident[:, :], start=True, stop=True)
                mm.then_inc(turn_mm, 1)

            def own_less_max(b, c):
                G = C * b + c
                pe.wait_ge(own_made, G + 1)
                pe.wait_ge(m_lo_made, G + 1)
                ps = ps_max[1][:, :]
                pe.matmul(ps, sum_spread[:, :], qk_hi[:, :], start=True, stop=False)
                pe.matmul(ps, sum_spread[:, :], qk_lo[:, :], start=False, stop=False)
                pe.matmul(ps, spread[:, :], m_neg[:, :], start=False, stop=True).then_inc(ow_mm, 1)

            def score_tile(b, g, i):
                T, r, j, t = TILES * (C * b + g) + i, g % 2, i // C, i % C
                if i == 0:
                    pe.wait_ge(m_landed[r], 2 * DMA * (2 * b + g // 2 + 1))
                wait(pe, p_hi_made, T - 1)
                pe.matmul(ps_score[i % 2][:, :], k_st[0:KS, r, j, P * t:P * (t + 1)], q_st[0:KS, r, j, :],
                          start=True, stop=True).then_inc(score_mm, 1)

            def value_tile(b, g, i):
                T, j, t = TILES * (C * b + g) + i, i // C, i % C
                if g == 0 and j == 0:
                    pe.wait_ge(v_lo_made, C * b + t + 1)
                if t == 0:
                    wait(pe, num_made, HG * (C * b + g) + j - 1)
                pe.wait_ge(p_lo_made, T + 1)
                ps, v = ps_av[j % 2][0:3 * DH, :], v_st[:, t, HG * g + j, :]
                pe.matmul(ps, v, p_hi[:, i % 4], start=(t == 0), stop=False)
                pe.matmul(ps, v, p_lo[:, i % 4], start=False, stop=(t == C - 1)).then_inc(av_mm, 1)

            pe.wait_ge(w_lo_made, 3 * C)
            pe.wait_ge(bias_made, 1)
            for c in range(2):
                for n in range(4):
                    for third in range(3):
                        project(0, c, n, third)
            for n in range(TILES):
                max_tile(0, 0, n)
            own_scores(0, 0)
            turn_max(0, 0)
            own_less_max(0, 0)

            def batch(b, first, last):
                for g in range(C):
                    nxt, nxt2 = after(b, g, 1), after(b, g, 2)
                    more = not (last and g >= 2)
                    bound = not (last and g == C - 1)
                    for i in range(TILES):
                        score_tile(b, g, i)
                        if bound:
                            for n in tiles_of_max(i):
                                max_tile(*nxt, n)
                        if i == LAG - 1 and not (first and g == 0):
                            value_tile(*after(b, g, -1), TILES - 1)
                        if g == 0 and 1 <= i < 1 + C:
                            values(b, i - 1)
                        if more and i >= 4:
                            project(*nxt2, (i - 4) // 3, (i - 4) % 3)
                        if bound and i == 10:
                            own_scores(*nxt)
                            turn_max(*nxt)
                        if bound and i == 14:
                            own_less_max(*nxt)
                        if i >= LAG:
                            value_tile(b, g, i - LAG)
                        elif i < LAG - 1 and not (first and g == 0):
                            value_tile(*after(b, g, -1), TILES - LAG + i)

            batches(pe, batch)
            for i in range(TILES - LAG, TILES):
                value_tile(B - 1, C - 1, i)

            pe.wait_ge(small_landed, 4 * DMA)
            pe.wait_ge(wide_landed[0], DMA)
            for c in range(C):
                for k in range(C):
                    mm = pe.matmul(ps_proj[0][:, c:c + 1], wide_view(0)[:, k, P * c:P * (c + 1)], bv_col[:, k:k + 1],
                                   start=(k == 0), stop=(k == C - 1))
            mm.then_inc(bo_mm, 1)

            def out_project(b, c):
                n = C * b + c
                pe.wait_ge(a_lo_made, C * (b + 1))
                wait(pe, y_f_made, n - 1)
                at = slice(P * c, P * (c + 1))
                for k in range(C):
                    mm = three(ps_proj[c % 2][:, :], (wo_hi[:, k, at], wo_lo[:, k, at]), (a_hi[:, k], a_lo[:, k]),
                               k == 0, k == C - 1)
                mm.then_inc(o_mm, 1)

            def hidden(b, m, ks):
                n = KH * b + m
                if ks[0] == 0:
                    wait(pe, h_hi_made, n - 1)
                at = slice(P * m, P * (m + 1))
                for k in ks:
                    if m < 2:
                        pe.wait_ge(y_lo_made, C * b + k + 1)
                    mm = three(ps_av[m % 2][:, :], (w1_hi[:, k, at], w1_lo[:, k, at]), (y_hi[:, k], y_lo[:, k]),
                               k == 0, k == C - 1)
                if ks[-1] == C - 1:
                    mm.then_inc(h_mm, 1)

            def outputs(b, m):
                pe.wait_ge(h_lo_made, KH * b + m + 1)
                for c in range(C):
                    at = slice(P * c, P * (c + 1))
                    left = (w2_hi[:, m, at], w2_lo[:, m, at]) if c < CS else (we_hi[:, m], we_lo[:, m])
                    if m == 0:
                        wait(pe, z_a_made, C * (b - 1) + c + 1)
                    if c == CS and m % 4 == 0:
                        pe.wait_ge(we_lo_made, 4 * b + m // 4 + 1)
                    mm = three(ps_out[c][:, :], left, (h_hi[:, m % 2], h_lo[:, m % 2]), m == 0, m == KH - 1)
                mm.then_inc(out_mm, 1)

            pe.wait_ge(wide_lo_made, len(wide_pieces))
            pe.wait_ge(bo_made, 1)
            for c in range(C):
                out_project(0, c)

            def rows(b, first, last):
                for m in range(2):
                    hidden(b, m, range(C - 1))
                for m in range(2):
                    hidden(b, m, range(C - 1, C))
                for m in range(KH):
                    if m + 2 < KH:
                        hidden(b, m + 2, range(C))
                    outputs(b, m)
                if not last:
                    for c in range(C):
                        out_project(b + 1, c)

            batches(pe, rows)


_INS = ['x', 'fside_BxSxS_0', 'itok_B_18_1004', 'itok_B_0_7', 'L0_cond_Wq', 'L0_cond_bq', 'L0_cond_Wk', 'L0_cond_bk',
        'L0_cond_Wv', 'L0_cond_bv', 'L0_cond_Wo', 'L0_cond_bo', 'L0_cond_b_prev', 'L0_cond_b_self',
        'L1_cond_W1', 'L1_cond_b1', 'L1_cond_W2', 'L1_cond_b2', 'L1_cond_We', 'L1_cond_be']


def kernel(**inputs):
    import numpy as _np
    import concourse.bacc as _bacc
    from concourse import mybir as _mybir
    from concourse.bass_utils import run_bass_kernel_spmd as _run

    nc = _bacc.Bacc("TRN2", target_bir_lowering=False, num_devices=1)
    arrays, args = {}, []
    for name in _INS:
        a = _np.ascontiguousarray(inputs[name])
        arrays[f"in_{name}_dram"] = a
        args.append(nc.dram_tensor(f"in_{name}_dram", a.shape, _mybir.dt.from_np(a.dtype), kind="ExternalInput").ap())
    out = nc.dram_tensor("out_dram", inputs["x"].shape, _mybir.dt.float32, kind="ExternalOutput").ap()
    cond_resid_program(nc, *args, out)
    r = _run(nc, [arrays], core_ids=[0])
    return r.results[0]["out_dram"]
```

```python
import concourse.bass as bass
from concourse import mybir
from contextlib import ExitStack

F32 = mybir.dt.float32
F32R = mybir.dt.float32r
I32 = mybir.dt.int32
ALU = mybir.AluOpType
ACT = mybir.ActivationFunctionType
AX = mybir.AxisListType


MASKED = -(2.0 ** 100)
DMA = 16


def cond_resid_program(nc, x, seq2, prev_len, expert, Wq, bq, Wk, bk, Wv, bv, Wo, bo, b_prev, b_self,
                       W1, b1, W2, b2, We, be, out):
    B, S, D = x.shape
    P = 128
    C = D // P
    DH = 32
    HG = P // DH
    H = D // DH
    HID = W1.shape[1]
    KH = HID // P
    CS = W2.shape[1] // P
    SCALE = float(DH) ** -0.5
    TILES = HG * C
    LAG = 3
    KM = 3 * DH + 1
    KS = KM + 2
    KE = DH + HG
    QUAD = 32
    assert (S, D, C, HG, H, KH, CS) == (512, 512, 4, 4, 16, 16, 3) and We.shape[2] == P

    attn_dram = nc.dram_tensor("attn_scratch", (B, C, P, S), F32, kind="Internal").ap()
    mask_dram = nc.dram_tensor("mask_scratch", (B, S), F32, kind="Internal").ap()

    keep = ExitStack()

    def sem(name):
        return keep.enter_context(nc.semaphore(name))

    def wait(eng, s, n):
        if not isinstance(n, int) or n > 0:
            eng.wait_ge(s, n)

    def f(ap):
        return ap.bitcast(F32)

    with keep:
        ps_score = [keep.enter_context(nc.psum_tensor(f"ps_score{i}", [P, 512], F32)) for i in range(2)]
        ps_max = [keep.enter_context(nc.psum_tensor(f"ps_max{i}", [P, 512], F32)) for i in range(2)]
        ps_av = [keep.enter_context(nc.psum_tensor(f"ps_av{i}", [P, 512], F32)) for i in range(2)]
        ps_proj = [keep.enter_context(nc.psum_tensor(f"ps_proj{i}", [P, 512], F32)) for i in range(2)]

        def sb(name, shape, dt=F32):
            return keep.enter_context(nc.sbuf_tensor(name, shape, dt))

        ident = sb("ident", [P, P], F32R)
        bias_o = sb("bias_o", [P, C])
        bias_1 = sb("bias_1", [P, KH])
        bias_2 = sb("bias_2", [P, C])
        bv_col = sb("bv_col", [P, C])
        bo_col = sb("bo_col", [P, C])
        ids = sb("ids", [1, B], I32)

        one = ExitStack()

        def sb1(name, shape, dt=F32):
            return one.enter_context(nc.sbuf_tensor(name, shape, dt))

        w_hi = sb1("w_hi", [P, 3, C, D], F32R)
        w_lo = sb1("w_lo", [P, 3, C, D], F32R)
        in_hi = sb1("in_hi", [P, 2, C, S], F32R)
        in_lo = sb1("in_lo", [P, 2, C, S], F32R)
        parts = sb1("parts", [P, 4, S], F32R)
        k_lo, k_hi, q_hi, q_lo = (parts[:, n, :] for n in range(4))
        stacks = sb1("stacks", [P, 2, HG, 2, S], F32R)
        k_st, q_st = stacks[:, :, :, 0], stacks[:, :, :, 1]
        p_f = sb1("p_f", [P, 2, S])
        p_hi = sb1("p_hi", [P, 4, S], F32R)
        before = one.enter_context(ExitStack())
        ident_f = before.enter_context(nc.sbuf_tensor("ident_f", [P, P], F32))
        spread_f = before.enter_context(nc.sbuf_tensor("spread_f", [KE, P], F32))
        len_i = before.enter_context(nc.sbuf_tensor("len_i", [B, 1], I32))
        len_f = before.enter_context(nc.sbuf_tensor("len_f", [B, 1], F32))
        pos_i = before.enter_context(nc.sbuf_tensor("pos_i", [B, S], I32))
        pos_f = before.enter_context(nc.sbuf_tensor("pos_f", [B, S], F32))
        mask = before.enter_context(nc.sbuf_tensor("mask", [B, S], F32))
        w_raw = before.enter_context(nc.sbuf_tensor("w_raw", [P, 3, C, D], F32))
        before.close()
        p_lo = sb1("p_lo", [P, 4, S], F32R)
        v_st = sb1("v_st", [P, C, H, 3 * DH], F32R)
        raw = sb1("raw", [P, 4, S])
        turned = sb1("turned", [P, 2, S])
        q_f = sb1("q_f", [P, S])
        qk_f = sb1("qk_f", [P, S])
        qk_hi = sb1("qk_hi", [P, S], F32R)
        qk_lo = sb1("qk_lo", [P, S], F32R)
        m_row = sb1("m_row", [HG, S])
        m_neg = sb1("m_neg", [KE, S], F32R)
        m_col = sb1("m_col", [P, C, HG])
        sum_heads = sb1("sum_heads", [P, HG], F32R)
        sum_spread = sb1("sum_spread", [P, P], F32R)
        spread = sb1("spread", [KE, P], F32R)
        bias = sb1("bias", [P, 3, C])
        b_in = sb1("b_in", [P, C, 2])
        b_qk = sb1("b_qk", [P, 2, C])
        v2 = sb1("v2", [P, 4, S])
        num = sb1("num", [P, 2, S])
        den = sb1("den", [P, 2, S])
        one.close()

        two = ExitStack()

        def sb2(name, shape, dt=F32):
            return two.enter_context(nc.sbuf_tensor(name, shape, dt))

        wo_hi = sb2("wo_hi", [P, C, D], F32R)
        wo_lo = sb2("wo_lo", [P, C, D], F32R)
        w1_hi = sb2("w1_hi", [P, C, HID], F32R)
        w1_lo = sb2("w1_lo", [P, C, HID], F32R)
        a_raw = sb2("a_raw", [P, 2, S])
        x_raw = sb2("x_raw", [P, S])
        x_t = sb2("x_t", [P, S])
        a_hi = sb2("a_hi", [P, C, S], F32R)
        a_lo = sb2("a_lo", [P, C, S], F32R)
        y_hi = sb2("y_hi", [P, C, S], F32R)
        y_lo = sb2("y_lo", [P, C, S], F32R)
        y_f = sb2("y_f", [P, S])
        h_f = sb2("h_f", [P, S])
        h_hi = sb2("h_hi", [P, 2, S], F32R)
        h_lo = sb2("h_lo", [P, 2, S], F32R)
        we_raw = sb2("we_raw", [P, 4, P])
        staged = two.enter_context(ExitStack())
        w2_raw = staged.enter_context(nc.sbuf_tensor("w2_raw", [P, 2, 2, CS * P], F32))
        staged.close()
        z_f = sb2("z_f", [P, 2, S])
        z_t = sb2("z_t", [P, 2, S])
        w2_hi = sb2("w2_hi", [P, KH, CS * P], F32R)
        w2_lo = sb2("w2_lo", [P, KH, CS * P], F32R)
        we_hi = sb2("we_hi", [P, KH, P], F32R)
        we_lo = sb2("we_lo", [P, KH, P], F32R)
        two.close()

        in_landed = [sem(f"in_landed{i}") for i in range(4)]
        w_landed = [sem(f"w_landed{i}") for i in range(3)]
        b_in_landed = [sem(f"b_in_landed{i}") for i in range(2)]
        bias_landed = sem("bias_landed")
        len_landed = sem("len_landed")
        mask_made = sem("mask_made")
        mask_landed = sem("mask_landed")
        consts_made = sem("consts_made")
        w_hi_made = sem("w_hi_made")
        w_lo_made = sem("w_lo_made")
        bias_mm = sem("bias_mm")
        bias_made = sem("bias_made")
        zeros_made = sem("zeros_made")
        v_ones_made = sem("v_ones_made")
        ones_made = [sem(f"ones_made{r}") for r in range(2)]
        turn_made = sem("turn_made")
        in_hi_made = sem("in_hi_made")
        in_lo_made = sem("in_lo_made")
        q_mm, k_mm, v2_mm, k2_mm = sem("q_mm"), sem("k_mm"), sem("v2_mm"), sem("k2_mm")
        v_mm = sem("v_mm")
        q_f_made, q_hi_made, q_lo_made = sem("q_f_made"), sem("q_hi_made"), sem("q_lo_made")
        k_hi_made, k_lo_made = sem("k_hi_made"), sem("k_lo_made")
        v2_made = sem("v2_made")
        qk_f_made, qk_hi_made, qk_lo_made = sem("qk_f_made"), sem("qk_hi_made"), sem("qk_lo_made")
        v_hi_made, v_lo_made = sem("v_hi_made"), sem("v_lo_made")
        stacked = [[sem(f"stacked{r}_{j}") for j in range(HG)] for r in range(2)]
        max_mm, max_made = sem("max_mm"), sem("max_made")
        own_mm, own_made = sem("own_mm"), sem("own_made")
        turn_mm = sem("turn_mm")
        m_row_made, m_hi_made, m_lo_made = sem("m_row_made"), sem("m_hi_made"), sem("m_lo_made")
        m_landed = [sem(f"m_landed{r}") for r in range(2)]
        ow_mm, ow_made = sem("ow_mm"), sem("ow_made")
        score_mm = sem("score_mm")
        p_f_made, p_hi_made, p_lo_made = sem("p_f_made"), sem("p_hi_made"), sem("p_lo_made")
        av_mm = sem("av_mm")
        av_lo_made = sem("av_lo_made")
        ov_made = sem("ov_made")
        den_made, num_made = sem("den_made"), sem("num_made")
        joined, rden_made = sem("joined"), sem("rden_made")
        attn_made = sem("attn_made")
        attn_stored = [sem(f"attn_stored{r}") for r in range(2)]

        wide_landed = [sem(f"wide_landed{i}") for i in range(4)]
        wide_hi_made, wide_lo_made = sem("wide_hi_made"), sem("wide_lo_made")
        w2_landed = [sem(f"w2_landed{i}") for i in range(2)]
        w2_hi_made, w2_lo_made = sem("w2_hi_made"), sem("w2_lo_made")
        small_landed = sem("small_landed")
        ids_landed = sem("ids_landed")
        bo_mm, bo_made = sem("bo_mm"), sem("bo_made")
        be_landed = sem("be_landed")
        we_landed, we_hi_made, we_lo_made = sem("we_landed"), sem("we_hi_made"), sem("we_lo_made")
        a_landed = [sem(f"a_landed{i}") for i in range(2)]
        a_hi_made, a_lo_made = sem("a_hi_made"), sem("a_lo_made")
        x_landed, x_made = sem("x_landed"), sem("x_made")
        o_mm = sem("o_mm")
        y_f_made, y_hi_made, y_lo_made = sem("y_f_made"), sem("y_hi_made"), sem("y_lo_made")
        h_mm = sem("h_mm")
        h_f_made, h_hi_made, h_lo_made = sem("h_f_made"), sem("h_hi_made"), sem("h_lo_made")
        out_mm = sem("out_mm")
        z_made, z_t_made = sem("z_made"), sem("z_t_made")
        stored = [sem(f"stored{r}") for r in range(2)]

        block = keep.enter_context(nc.Block())

        def after(b, g, k):
            return b + (g + k) // C, (g + k) % C

        def stack_count(b, c):
            return DMA * (3 * (2 * b + c // 2 + 1) + b + 1)

        def tiles_of_max(i):
            ends = (2, 3, 5, 7, 8, 10, 12, 14, 14, TILES)
            return range(ends[i - 1] if i else 0, ends[i]) if i < len(ends) else range(0)

        turn_at = {(1, 6): (0,), (1, 7): (1,), (1, 11): (2,), (1, 12): (3,), (1, 14): (4,), (1, 15): (5,),
                   (2, 2): (6,), (2, 3): (7,)}
        in_hi_at = {(1, 10): (0,), (1, 11): (1,), (1, 12): (2,), (1, 13): (3,), (2, 0): (4,), (2, 2): (5,), (2, 4): (6,), (2, 5): (7,)}
        in_lo_at = {(1, 10): (0,), (1, 11): (1,), (1, 12): (2,), (1, 13): (3,), (2, 0): (4,), (2, 2): (5,), (2, 4): (6,), (2, 5): (7,)}

        WIDE = C + C * HID // S
        wide_at = {(2, i): (i - 8,) for i in range(8, TILES)}
        wide_at.update({(3, i): (i + TILES - 8,) for i in range(WIDE - TILES + 8)})
        attended_at = {(3, i): (i - 12,) for i in range(12, 12 + C)}

        def wide_source(n):
            if n < C:
                return Wo[P * n:P * (n + 1), :]
            k, at = (n - C) // (HID // S), (n - C) % (HID // S)
            return W1[P * k:P * (k + 1), S * at:S * (at + 1)]

        def wide_parts(n):
            if n < C:
                return wo_hi[:, n], wo_lo[:, n]
            k, at = (n - C) // (HID // S), (n - C) % (HID // S)
            return w1_hi[:, k, S * at:S * (at + 1)], w1_lo[:, k, S * at:S * (at + 1)]

        W2S = KH // 2

        def first_max(t):
            return range(TILES * t // (3 * C), TILES * (t + 1) // (3 * C))

        def blocks(t, b, c, q):
            return t[bass.ds(b, 1)].rearrange("o (tb ti) f -> (o ti) tb f", ti=QUAD)[
                :, :, c * P + QUAD * q:c * P + QUAD * (q + 1)]

        def batches(eng, run):
            run(0, True, False)
            with eng.Fori(1, B - 1) as b:
                run(b, False, False)
            run(B - 1, False, True)

        ps_out = ps_score + ps_max

        @block.sync
        def _(sp):
            def column(dst, src, landed):
                sp.dma_start(dst, src.rearrange("(c p) -> p c", p=P), allow_slow_non_contiguous=True).then_inc(landed, DMA)

            def weights(n):
                sp.dma_start(w_raw[:, n], (Wq, Wk, Wv)[n].rearrange("(c p) n -> p c n", p=P)).then_inc(w_landed[n], DMA)

            def load(b, j):
                k = 8 * b + j
                src = x if j < C else seq2
                wait(sp, turn_made, k - 3)
                for q in range(P // QUAD):
                    sp.dma_start(raw[QUAD * q:QUAD * (q + 1), j % 4].rearrange("p (tb f) -> p tb f", f=QUAD),
                                 blocks(src, b, j % C, q)).then_inc(in_landed[j % 4], DMA)

            def stack(b, c, j):
                G, r = C * b + c, c % 2
                if j == 0:
                    wait(sp, q_lo_made, G + 1)
                    wait(sp, k_lo_made, G + 1)
                wait(sp, score_mm, TILES * (G - 2) + C * (j + 1))
                if c < 2:
                    sp.dma_start(f(k_st[KM - 1:KM, r, j]), mask_dram[bass.ds(b, 1)]).then_inc(stacked[r][j], DMA)
                rows = slice(DH * j, DH * (j + 1))
                for n, pair in enumerate((parts[rows, 1:3], parts[rows, 0:3:2], parts[rows, 1:4:2])):
                    sp.dma_start(f(stacks[DH * n:DH * (n + 1), r, j]), f(pair)).then_inc(stacked[r][j], DMA)

            def store(b, c):
                wait(sp, attn_made, C * b + c + 1)
                sp.dma_start(attn_dram[bass.ds(b, 1), c].rearrange("o p s -> (o p) s"),
                             num[:, c % 2]).then_inc(attn_stored[c % 2], DMA)

            def wide(n):
                if n < 4:
                    sp.wait_ge(turn_made, 2 * C * B)
                else:
                    sp.wait_ge(wide_lo_made, n - 3)
                sp.dma_start(raw[:, n % 4], wide_source(n)).then_inc(wide_landed[n % 4], DMA)

            def attended(b, c):
                wait(sp, a_lo_made, C * b + c - 1)
                sp.dma_start(a_raw[:, c % 2], attn_dram[bass.ds(b, 1), c].rearrange("o p s -> (o p) s")).then_inc(a_landed[c % 2], DMA)

            def residual(b, c):
                wait(sp, x_made, C * b + c)
                for q in range(P // QUAD):
                    sp.dma_start(x_raw[QUAD * q:QUAD * (q + 1), :].rearrange("p (tb f) -> p tb f", f=QUAD),
                                 blocks(x, b, c, q)).then_inc(x_landed, DMA)

            weights(1)
            sp.dma_start(len_i[:, :], prev_len.rearrange("(b o) -> b o", o=1)).then_inc(len_landed, DMA)
            column(b_in[:, :, 0], b_prev.rearrange("a o d -> (a o d)"), b_in_landed[0])
            column(b_in[:, :, 1], b_self.rearrange("a o d -> (a o d)"), b_in_landed[1])
            for j in range(C):
                load(0, j)
            weights(0)
            column(b_qk[:, 0, :], bq, bias_landed)
            column(b_qk[:, 1, :], bk, bias_landed)
            for j in range(C, 2 * C):
                load(0, j)
            weights(2)
            sp.wait_ge(mask_made, 1)
            sp.dma_start(mask_dram, mask[:, :]).then_inc(mask_landed, DMA)
            sp.wait_ge(mask_landed, DMA)
            sp.wait_ge(ones_made[0], 1)
            for j in range(HG):
                stack(0, 0, j)
            sp.wait_ge(ones_made[1], 1)
            for j in range(HG):
                stack(0, 1, j)
            for dst, src in ((bv_col[:, :], bv), (bo_col[:, :], bo), (bias_1[:, :], b1), (bias_2[:, 0:CS], b2)):
                sp.dma_start(dst, src.rearrange("(c p) -> p c", p=P), allow_slow_non_contiguous=True).then_inc(small_landed, DMA)
            sp.dma_start(ids[:, :], expert.rearrange("(o b) -> o b", o=1)).then_inc(ids_landed, DMA)

            def batch(b, first, last):
                for g in range(C):
                    more = not (last and g >= 2)
                    if g == 1 and not last:
                        for j in range(C):
                            load(b + 1, j)
                    if more:
                        for j in range(HG):
                            if g == 1 and j % 2 == 0 and not last:
                                load(b + 1, C + j)
                                load(b + 1, C + j + 1)
                            stack(*after(b, g, 2), j)
                    if last and g == 2:
                        for n in range(10):
                            wide(n)
                    if last and g == 3:
                        for j in range(HG):
                            sp.wait_ge(stacked[1][j], stack_count(b, g))
                        for r in range(2):
                            sp.wait_ge(attn_stored[r], 2 * DMA)
                        residual(0, 0)
                        attended(0, 0)
                        attended(0, 1)
                        for n in range(10, WIDE):
                            wide(n)
                        attended(0, 2)
                        attended(0, 3)
                    if not (first and g == 0):
                        store(*after(b, g, -1))

            batches(sp, batch)

            def w2_piece(n):
                wait(sp, w2_lo_made, n - 1)
                sp.dma_start(w2_raw[:, n % 2], W2.rearrange("(k p) n -> p k n", p=P)[:, 2 * n:2 * n + 2]).then_inc(w2_landed[n % 2], DMA)

            def expert_weights(b, j):
                e = sp.value_load(ids[0:1, bass.ds(b, 1)], min_val=0, max_val=We.shape[0] - 1)
                src = We[bass.ds(e, 1)].rearrange("o (k p) n -> p (o k) n", p=P)[:, 4 * j:4 * j + 4]
                wait(sp, we_lo_made, 4 * b + j)
                sp.dma_start(we_raw[:, :, :], src).then_inc(we_landed, DMA)

            def expert_bias(b):
                e = sp.value_load(ids[0:1, bass.ds(b, 1)], min_val=0, max_val=be.shape[0] - 1)
                wait(sp, z_made, C * b)
                sp.dma_start(bias_2[:, CS:C], be[bass.ds(e, 1)].rearrange("o p -> p o"), allow_slow_non_contiguous=True).then_inc(be_landed, DMA)

            def result(b, c):
                sp.wait_ge(z_t_made, C * b + c + 1)
                for q in range(P // QUAD):
                    sp.dma_start(blocks(out, b, c, q),
                                 z_t[QUAD * q:QUAD * (q + 1), c % 2].rearrange("p (tb f) -> p tb f", f=QUAD)
                                 ).then_inc(stored[c % 2], DMA)

            sp.wait_ge(ids_landed, DMA)
            sp.wait_ge(av_mm, TILES * C * B)
            expert_weights(0, 0)
            w2_piece(0)
            w2_piece(1)
            expert_bias(0)
            residual(0, 1)
            store(B - 1, C - 1)
            residual(0, 2)
            residual(0, 3)
            w2_piece(2)
            expert_weights(0, 1)
            w2_piece(3)
            expert_weights(0, 2)
            for n in range(4, W2S):
                w2_piece(n)
            for r in range(2):
                sp.wait_ge(attn_stored[r], DMA * C * B // 2)

            def rows(b, first, last):
                expert_weights(b, 3)
                if not last:
                    attended(b + 1, 0)
                    attended(b + 1, 1)
                    expert_weights(b + 1, 0)
                    attended(b + 1, 2)
                    attended(b + 1, 3)
                    residual(b + 1, 0)
                    expert_weights(b + 1, 1)
                    expert_weights(b + 1, 2)
                    for c in range(1, C):
                        residual(b + 1, c)
                for c in range(C):
                    result(b, c)
                if not last:
                    expert_bias(b + 1)

            batches(sp, rows)
            for r in range(2):
                sp.wait_ge(stored[r], (P // QUAD) * DMA * C * B // 2)

        @block.gpsimd
        def _(pool):
            pool.memset(ident_f[:, :], 0.0).then_inc(consts_made, 1)
            pool.memset(spread_f[:, :], 0.0).then_inc(consts_made, 1)
            pool.iota(pos_i[:, :], pattern=[[1, S]], base=0, channel_multiplier=0).then_inc(consts_made, 1)
            pool.wait_ge(consts_made, 2)
            pool.affine_select(out=ident_f[:, :], in_=ident_f[:, :], compare_op=ALU.not_equal, fill=1.0, base=0,
                               pattern=[[-1, P]], channel_multiplier=1).then_inc(consts_made, 1)
            for n in range(2):
                pool.wait_ge(consts_made, 4 + n)
                pool.affine_select(out=spread_f[:, :].rearrange("k (j d) -> k j d", d=DH),
                                   in_=spread_f[:, :].rearrange("k (j d) -> k j d", d=DH),
                                   compare_op=ALU.not_equal, fill=1.0, base=-QUAD * n,
                                   pattern=[[-1, HG], [0, DH]], channel_multiplier=1).then_inc(consts_made, 1)

            pool.memset(f(stacks[KM - 1:KS, 1]), 1.0).then_inc(ones_made[1], 1)
            pool.wait_ge(ones_made[1], 1)

            def p_low(b, g, i):
                T = TILES * (C * b + g) + i
                pool.wait_ge(p_hi_made, T + 1)
                pool.tensor_tensor(p_lo[:, i % 4], p_f[:, i % 2], f(p_hi[:, i % 4]),
                                   ALU.subtract).then_inc(p_lo_made, 1)

            def own_value(b, c):
                G = C * b + c
                pool.wait_ge(ow_made, G + 1)
                pool.wait_ge(v2_made, G + 1)
                pool.tensor_tensor(v2[:, c], v2[:, c], den[:, c % 2], ALU.mult).then_inc(ov_made, 1)

            def add_own(b, c):
                G, r = C * b + c, c % 2
                pool.wait_ge(num_made, HG * (G + 1))
                pool.wait_ge(ov_made, G + 1)
                pool.tensor_tensor(num[:, r], num[:, r], v2[:, c], ALU.add).then_inc(joined, 1)

            def in_low(b, j):
                pool.wait_ge(in_hi_made, 2 * C * b + j + 1)
                at = (1 - j // C, j % C)
                pool.tensor_tensor(in_lo[:, at[0], at[1]], turned[:, j % 2], f(in_hi[:, at[0], at[1]]),
                                   ALU.subtract).then_inc(in_lo_made, 1)

            for j in range(2 * C):
                in_low(0, j)
            pool.wait_ge(w_lo_made, 3 * C)
            pool.wait_ge(bias_mm, 2)
            pool.memset(f(v_st[:, :, :, 2 * DH:3 * DH]), 1.0).then_inc(v_ones_made, 1)
            pool.wait_ge(v_ones_made, 1)


            def batch(b, first, last):
                for g in range(C):
                    for i in range(TILES):
                        p_low(b, g, i)
                        if not last:
                            for j in in_lo_at.get((g, i), ()):
                                in_low(b + 1, j)
                        if i == 6:
                            own_value(b, g)
                        if i == 7 and not (first and g == 0):
                            add_own(*after(b, g, -1))

            batches(pool, batch)
            add_own(B - 1, C - 1)

        @block.scalar
        def _(act):
            def weights_high(n):
                act.wait_ge(w_landed[n], DMA)
                for c in range(C):
                    act.copy(w_hi[:, n, c], w_raw[:, n, c]).then_inc(w_hi_made, 1)

            def in_high(b, j):
                k = 2 * C * b + j
                act.wait_ge(turn_made, k + 1)
                wait(act, k_mm if j < C else v2_mm, C * b)
                act.copy(in_hi[:, 1 - j // C, j % C], turned[:, j % 2]).then_inc(in_hi_made, 1)

            def q_out(b, c):
                G = C * b + c
                act.wait_ge(q_mm, G + 1)
                wait(act, qk_f_made, G)
                act.activation(q_f[:, :], ps_proj[0][:, :], ACT.Identity,
                               bias=bias[:, 0, c:c + 1]).then_inc(q_f_made, 1)
                act.activation(q_hi[:, :], ps_proj[0][:, :], ACT.Identity,
                               bias=bias[:, 0, c:c + 1]).then_inc(q_hi_made, 1)

            def k_out(b, c):
                act.wait_ge(k_mm, C * b + c + 1)
                pb, pc = after(b, c, -1)
                for j in range(HG):
                    wait(act, stacked[pc % 2][j], stack_count(pb, pc))
                act.activation(k_hi[:, :], ps_proj[1][:, :], ACT.Identity,
                               bias=bias[:, 1, c:c + 1]).then_inc(k_hi_made, 1)

            def v2_out(b, c):
                G = C * b + c
                act.wait_ge(v2_mm, G + 1)
                wait(act, attn_made, G - 3)
                act.copy(v2[:, c], ps_proj[0][:, :]).then_inc(v2_made, 1)

            def qk_high(b, c):
                G = C * b + c
                act.wait_ge(qk_f_made, G + 1)
                wait(act, ow_mm, G)
                act.copy(qk_hi[:, :], qk_f[:, :]).then_inc(qk_hi_made, 1)

            def v_high(b, t):
                act.wait_ge(v_mm, C * b + t + 1)
                wait(act, av_mm, C * TILES * b)
                act.copy(v_st[:, t, :, 0:DH],
                         ps_proj[1 - t % 2][:, :].rearrange("p (h d) -> p h d", d=DH)).then_inc(v_hi_made, 1)

            def own_row(b, c):
                G = C * b + c
                act.wait_ge(own_mm, G + 1)
                wait(act, m_lo_made, G)
                act.copy(m_row[:, :], ps_max[1][0:HG, :]).then_inc(own_made, 1)

            def m_high(b, c):
                G = C * b + c
                act.wait_ge(m_row_made, G + 1)
                pb, pc = after(b, c, -1)
                wait(act, m_landed[pc % 2], 2 * DMA * (2 * pb + pc // 2 + 1))
                wait(act, ow_mm, G)
                act.mul(m_neg[0:HG, :], m_row[:, :], -1.0).then_inc(m_hi_made, 1)

            def maxima(b, c):
                G, r = C * b + c, c % 2
                wait(act, m_lo_made, G + 1)
                for n in range(2):
                    act.dma_start(f(q_st[KM + n:KM + n + 1, r]),
                                  f(m_neg[QUAD * n:QUAD * n + HG])).then_inc(m_landed[r], DMA)

            def own_weight(b, c):
                G = C * b + c
                act.wait_ge(ow_mm, G + 1)
                wait(act, attn_made, G - 1)
                act.activation(den[:, c % 2], ps_max[1][:, :], ACT.Exp, scale=SCALE).then_inc(ow_made, 1)

            def probabilities(b, g, i):
                T = TILES * (C * b + g) + i
                act.wait_ge(score_mm, T + 1)
                wait(act, p_lo_made, T - 1)
                act.activation(p_f[:, i % 2], ps_score[i % 2][:, :], ACT.Exp, scale=SCALE).then_inc(p_f_made, 1)
                wait(act, av_mm, T - 3)
                act.activation(p_hi[:, i % 4], ps_score[i % 2][:, :], ACT.Exp, scale=SCALE).then_inc(p_hi_made, 1)

            def av_low(b, g, j):
                Hd = HG * (C * b + g) + j
                act.wait_ge(av_mm, C * (Hd + 1))
                if j == 0:
                    wait(act, attn_stored[g % 2], DMA * (2 * b + g // 2))
                act.copy(num[DH * j:DH * (j + 1), g % 2], ps_av[j % 2][DH:2 * DH, :]).then_inc(av_lo_made, 1)

            def wide_high(n):
                act.wait_ge(wide_landed[n % 4], DMA * (n // 4 + 1))
                if n == 0:
                    act.wait_ge(v2_mm, C * B)
                act.copy(wide_parts(n)[0], raw[:, n % 4]).then_inc(wide_hi_made, 1)

            def attended_high(b, c):
                act.wait_ge(a_landed[c % 2], DMA * (2 * b + c // 2 + 1))
                wait(act, o_mm, C * b)
                act.copy(a_hi[:, c], a_raw[:, c % 2]).then_inc(a_hi_made, 1)

            weights_high(1)
            for j in range(C):
                in_high(0, j)
            weights_high(0)
            for j in range(C, 2 * C):
                in_high(0, j)
            act.wait_ge(bias_made, 1)
            k_out(0, 0)
            act.wait_ge(bias_made, 2)
            q_out(0, 0)
            weights_high(2)
            qk_high(0, 0)
            v2_out(0, 0)
            k_out(0, 1)
            q_out(0, 1)
            v2_out(0, 1)
            own_row(0, 0)
            v_high(0, 0)
            m_high(0, 0)
            v_high(0, 1)
            maxima(0, 0)
            v_high(0, 2)
            own_weight(0, 0)
            v_high(0, 3)

            def batch(b, first, last):
                for g in range(C):
                    nxt, nxt2 = after(b, g, 1), after(b, g, 2)
                    project = not (last and g >= 2)
                    maximum = not (last and g == C - 1)
                    for i in range(TILES):
                        if i == 11 and maximum:
                            own_row(*nxt)
                        if i == 15 and maximum:
                            own_weight(*nxt)
                        probabilities(b, g, i)
                        if i == 0 and not (first and g == 0):
                            av_low(*after(b, g, -1), HG - 2)
                        if i == 0 and maximum and not (first and g == 0):
                            v2_out(*nxt)
                        if i == 1 and maximum:
                            qk_high(*nxt)
                        if i == 3 and not (first and g == 0):
                            av_low(*after(b, g, -1), HG - 1)
                        if g == 0 and not first and 2 <= i < 2 + C:
                            v_high(b, i - 2)
                        if not last:
                            for j in in_hi_at.get((g, i), ()):
                                in_high(b + 1, j)
                        if i == 7 and project:
                            k_out(*nxt2)
                        if i == 8:
                            av_low(b, g, 0)
                        if i == 10 and project:
                            q_out(*nxt2)
                        if i == 11 and maximum:
                            m_high(*nxt)
                        if i == 12:
                            av_low(b, g, 1)
                        if i == 12 and maximum:
                            maxima(*nxt)
                        if last:
                            for n in wide_at.get((g, i), ()):
                                wide_high(n)
                            for c in attended_at.get((g, i), ()):
                                attended_high(0, c)

            batches(act, batch)
            av_low(B - 1, C - 1, HG - 2)
            av_low(B - 1, C - 1, HG - 1)

            def w2_high(n):
                act.wait_ge(w2_landed[n % 2], DMA * (n // 2 + 1))
                if n == 0:
                    act.wait_ge(wide_lo_made, WIDE)
                act.copy(w2_hi[:, 2 * n:2 * n + 2], w2_raw[:, n % 2]).then_inc(w2_hi_made, 1)

            def expert_high(b, j):
                act.wait_ge(we_landed, DMA * (4 * b + j + 1))
                wait(act, out_mm, KH * (b - 1) + 4 * j + 4)
                act.copy(we_hi[:, 4 * j:4 * j + 4], we_raw[:, :, :]).then_inc(we_hi_made, 1)

            def y_high(b, c):
                act.wait_ge(y_f_made, C * b + c + 1)
                wait(act, h_mm, KH * b)
                act.copy(y_hi[:, c], y_f[:, :]).then_inc(y_hi_made, 1)

            def hidden(b, m):
                n = KH * b + m
                act.wait_ge(h_mm, n + 1)
                wait(act, h_lo_made, n)
                act.activation(h_f[:, :], ps_av[m % 2][:, :], ACT.Gelu, bias=bias_1[:, m:m + 1]).then_inc(h_f_made, 1)
                wait(act, out_mm, n - 1)
                act.activation(h_hi[:, m % 2], ps_av[m % 2][:, :], ACT.Gelu, bias=bias_1[:, m:m + 1]).then_inc(h_hi_made, 1)

            def result(b, c):
                n = C * b + c
                act.wait_ge(out_mm, KH * (b + 1))
                if c == CS:
                    act.wait_ge(be_landed, DMA * (b + 1))
                wait(act, z_t_made, n - 1)
                act.activation(z_f[:, c % 2], ps_out[c][:, :], ACT.Identity, bias=bias_2[:, c:c + 1]).then_inc(z_made, 1)

            act.wait_ge(small_landed, 4 * DMA)
            w2_high(0)
            y_high(0, 0)
            y_high(0, 1)
            w2_high(1)
            y_high(0, 2)
            y_high(0, 3)
            for r in range(2):
                act.wait_ge(attn_stored[r], DMA * C * B // 2)
            expert_high(0, 0)

            def rows(b, first, last):
                for m in range(KH):
                    hidden(b, m)
                    if first and m < 2:
                        w2_high(2 + m)
                        expert_high(b, m + 1)
                    if m == 4:
                        expert_high(b, 3)
                    if first and 2 <= m < W2S - 2:
                        w2_high(2 + m)
                    if not last and m in (6, 10, 14):
                        expert_high(b + 1, m // 4 - 1)
                    if not last and 3 <= m < 3 + C:
                        attended_high(b + 1, m - 3)
                    if not last and m == KH - 2:
                        y_high(b + 1, 0)
                if not last:
                    for c in range(1, C):
                        y_high(b + 1, c)
                for c in range(C):
                    result(b, c)

            batches(act, rows)

        @block.vector
        def _(dve):
            dve.memset(f(sum_heads[:, :]), 0.0).then_inc(zeros_made, 1)
            dve.memset(f(sum_spread[:, :]), 0.0).then_inc(zeros_made, 1)
            dve.memset(f(m_neg[:, :]), 0.0).then_inc(zeros_made, 1)
            dve.memset(f(stacks[KM - 1:KS, 0]), 1.0).then_inc(ones_made[0], 1)
            dve.wait_ge(zeros_made, 3)
            for j in range(HG):
                rows = slice(DH * j, DH * (j + 1))
                dve.memset(f(sum_heads[rows, j:j + 1]), 1.0).then_inc(zeros_made, 1)
                dve.memset(f(sum_spread[rows, rows]), 1.0).then_inc(zeros_made, 1)
            dve.wait_ge(consts_made, 6)
            dve.tensor_copy(ident[:, :], ident_f[:, :]).then_inc(zeros_made, 1)
            dve.tensor_copy(spread[:, :], spread_f[:, :]).then_inc(zeros_made, 1)

            dve.wait_ge(len_landed, DMA)
            dve.tensor_copy(len_f[:, :], len_i[:, :]).then_inc(zeros_made, 1)
            dve.tensor_copy(pos_f[:, :], pos_i[:, :]).then_inc(zeros_made, 1)
            dve.wait_ge(zeros_made, 3 + 2 * HG + 4)
            dve.tensor_scalar(mask[:, :], pos_f[:, :], len_f[:, 0:1], MASKED, ALU.is_ge, ALU.mult).then_inc(mask_made, 1)

            def weights_low(n, done):
                for c in range(C):
                    dve.wait_ge(w_hi_made, C * done + c + 1)
                    dve.tensor_tensor(w_lo[:, n, c], w_raw[:, n, c], f(w_hi[:, n, c]), ALU.subtract).then_inc(w_lo_made, 1)

            def turn(b, j):
                k = 2 * C * b + j
                dve.wait_ge(in_landed[j % 4], (P // QUAD) * DMA * (2 * b + j // 4 + 1))
                wait(dve, in_lo_made, k - 1)
                dve.transpose(turned[:, j % 2], raw[:, j % 4]).then_inc(turn_made, 1)

            def q_low(b, c):
                dve.wait_ge(q_hi_made, C * b + c + 1)
                dve.tensor_tensor(q_lo[:, :], q_f[:, :], f(q_hi[:, :]), ALU.subtract).then_inc(q_lo_made, 1)

            def k_low(b, c):
                dve.wait_ge(k_hi_made, C * b + c + 1)
                dve.scalar_tensor_tensor(out=k_lo[:, :], in0=ps_proj[1][:, :], scalar=bias[:, 1, c:c + 1],
                                         in1=f(k_hi[:, :]), op0=ALU.add, op1=ALU.subtract).then_inc(k_lo_made, 1)

            def qk(b, c):
                G = C * b + c
                dve.wait_ge(k2_mm, G + 1)
                dve.wait_ge(q_hi_made, G + 1)
                wait(dve, qk_lo_made, G)
                dve.scalar_tensor_tensor(out=qk_f[:, :], in0=ps_proj[1][:, :], scalar=bias[:, 2, c:c + 1],
                                         in1=q_f[:, :], op0=ALU.add, op1=ALU.mult).then_inc(qk_f_made, 1)

            def qk_low(b, c):
                dve.wait_ge(qk_hi_made, C * b + c + 1)
                dve.tensor_tensor(qk_lo[:, :], qk_f[:, :], f(qk_hi[:, :]), ALU.subtract).then_inc(qk_lo_made, 1)

            def v_low(b, t):
                dve.wait_ge(v_hi_made, C * b + t + 1)
                dve.tensor_tensor(v_st[:, t, :, DH:2 * DH], ps_proj[1 - t % 2][:, :].rearrange("p (h d) -> p h d", d=DH),
                                  f(v_st[:, t, :, 0:DH]), ALU.subtract).then_inc(v_lo_made, 1)

            def maximum(b, c, n):
                G = C * b + c
                dve.wait_ge(max_mm, TILES * G + n + 1)
                if n == 0:
                    wait(dve, turn_mm, G)
                dve.tensor_reduce(m_col[:, n % C, n // C:n // C + 1], ps_max[n % 2][:, :], AX.X,
                                  ALU.max).then_inc(max_made, 1)

            def max_row(b, c):
                G = C * b + c
                dve.wait_ge(own_made, G + 1)
                dve.wait_ge(turn_mm, G + 1)
                dve.tensor_tensor(m_row[:, :], ps_max[0][0:HG, :], m_row[:, :], ALU.max).then_inc(m_row_made, 1)

            def m_low(b, c):
                dve.wait_ge(m_hi_made, C * b + c + 1)
                dve.scalar_tensor_tensor(out=m_neg[QUAD:QUAD + HG, :], in0=m_row[:, :], scalar=-1.0,
                                         in1=f(m_neg[0:HG, :]), op0=ALU.mult, op1=ALU.subtract).then_inc(m_lo_made, 1)

            def head(b, g, j):
                G = C * b + g
                Hd = HG * G + j
                rows = slice(DH * j, DH * (j + 1))
                dve.wait_ge(ov_made, G + 1)
                dve.wait_ge(av_lo_made, Hd + 1)
                dve.tensor_tensor(den[rows, g % 2], ps_av[j % 2][2 * DH:3 * DH, :], den[rows, g % 2],
                                  ALU.add).then_inc(den_made, 1)
                dve.tensor_tensor(num[rows, g % 2], ps_av[j % 2][0:DH, :], num[rows, g % 2],
                                  ALU.add).then_inc(num_made, 1)

            def wide_low(n):
                hi, lo = wide_parts(n)
                dve.wait_ge(wide_hi_made, n + 1)
                dve.tensor_tensor(lo, raw[:, n % 4], f(hi), ALU.subtract).then_inc(wide_lo_made, 1)

            def attended_low(b, c):
                dve.wait_ge(a_hi_made, C * b + c + 1)
                dve.tensor_tensor(a_lo[:, c], a_raw[:, c % 2], f(a_hi[:, c]), ALU.subtract).then_inc(a_lo_made, 1)

            def turn_x(b, c):
                n = C * b + c
                dve.wait_ge(x_landed, (P // QUAD) * DMA * (n + 1))
                wait(dve, y_f_made, n)
                dve.transpose(x_t[:, :], x_raw[:, :]).then_inc(x_made, 1)

            def one_over_den(b, g, n):
                G, r = C * b + g, g % 2
                dve.wait_ge(den_made, HG * (G + 1))
                at = slice(S // 4 * n, S // 4 * (n + 1))
                dve.reciprocal(den[:, r, at], den[:, r, at]).then_inc(rden_made, 1)

            def normalize(b, g):
                G, r = C * b + g, g % 2
                dve.wait_ge(rden_made, 4 * (G + 1))
                dve.wait_ge(joined, G + 1)
                dve.tensor_tensor(num[:, r], num[:, r], den[:, r], ALU.mult).then_inc(attn_made, 1)

            def bias_sums(w):
                cols = ps_av[w][:, 0:2 * C].rearrange("p (c s) -> p c s", s=2)
                for n, s in ((0, 1),) if w == 0 else ((1, 0), (2, 1)):
                    last = dve.tensor_tensor(bias[:, n, :], cols[:, :, s], b_qk[:, w, :], ALU.add)
                last.then_inc(bias_made, 1)

            weights_low(1, 0)
            for j in range(C):
                turn(0, j)
            dve.wait_ge(bias_landed, 2 * DMA)
            dve.wait_ge(bias_mm, 1)
            bias_sums(1)
            weights_low(0, 1)
            for j in range(C, 2 * C):
                turn(0, j)
            dve.wait_ge(bias_mm, 2)
            bias_sums(0)
            k_low(0, 0)
            q_low(0, 0)
            qk(0, 0)
            weights_low(2, 2)
            qk_low(0, 0)
            for t in range(3 * C):
                for n in first_max(t):
                    maximum(0, 0, n)
                if t == 4:
                    k_low(0, 1)
                if t == 8:
                    q_low(0, 1)
            qk(0, 1)
            max_row(0, 0)
            v_low(0, 0)
            m_low(0, 0)
            for t in range(1, C):
                v_low(0, t)

            def batch(b, first, last):
                for g in range(C):
                    nxt, nxt2 = after(b, g, 1), after(b, g, 2)
                    project = not (last and g >= 2)
                    bound = not (last and g == C - 1)
                    started = not (first and g == 0)
                    for i in range(TILES):
                        if bound:
                            for n in tiles_of_max(i):
                                maximum(*nxt, n)
                        if g == 0 and not first and 2 <= i < 2 + C:
                            v_low(b, i - 2)
                        if i == 1 and started:
                            head(*after(b, g, -1), HG - 2)
                        if i == 5 and bound:
                            qk_low(*nxt)
                        if i == 4 and started:
                            head(*after(b, g, -1), HG - 1)
                        if not last:
                            for j in turn_at.get((g, i), ()):
                                turn(b + 1, j)
                        if i == 8 and project:
                            k_low(*nxt2)
                        if i == 8:
                            head(b, g, 0)
                        if i == 11 and bound:
                            max_row(*nxt)
                        if i == 11 and project:
                            q_low(*nxt2)
                        if i == 11 and bound:
                            m_low(*nxt)
                        if i in (10, 13) and started:
                            for n in range(2) if i == 10 else range(2, 4):
                                one_over_den(*after(b, g, -1), n)
                        if i == 13 and project:
                            qk(*nxt2)
                        if i == 12:
                            head(b, g, 1)
                        if i == 14 and started:
                            normalize(*after(b, g, -1))
                        if last:
                            for n in wide_at.get((g, i), ()):
                                wide_low(n)
                            for c in attended_at.get((g, i), ()):
                                attended_low(0, c)

            batches(dve, batch)

            def w2_low(n):
                at = slice(2 * n, 2 * n + 2)
                dve.wait_ge(w2_hi_made, n + 1)
                dve.tensor_tensor(w2_lo[:, at], w2_raw[:, n % 2], f(w2_hi[:, at]), ALU.subtract).then_inc(w2_lo_made, 1)

            def expert_low(b, j):
                dve.wait_ge(we_hi_made, 4 * b + j + 1)
                dve.tensor_tensor(we_lo[:, 4 * j:4 * j + 4], we_raw[:, :, :], f(we_hi[:, 4 * j:4 * j + 4]),
                                  ALU.subtract).then_inc(we_lo_made, 1)

            def y_out(b, c):
                n = C * b + c
                dve.wait_ge(o_mm, n + 1)
                dve.wait_ge(x_made, n + 1)
                wait(dve, y_lo_made, n)
                dve.scalar_tensor_tensor(out=y_f[:, :], in0=ps_proj[c % 2][:, :], scalar=bias_o[:, c:c + 1],
                                         in1=x_t[:, :], op0=ALU.add, op1=ALU.add).then_inc(y_f_made, 1)

            def y_low(b, c):
                dve.wait_ge(y_hi_made, C * b + c + 1)
                dve.tensor_tensor(y_lo[:, c], y_f[:, :], f(y_hi[:, c]), ALU.subtract).then_inc(y_lo_made, 1)

            def hidden_low(b, m):
                dve.wait_ge(h_hi_made, KH * b + m + 1)
                dve.tensor_tensor(h_lo[:, m % 2], h_f[:, :], f(h_hi[:, m % 2]), ALU.subtract).then_inc(h_lo_made, 1)

            def turn_result(b, c):
                dve.wait_ge(z_made, C * b + c + 1)
                wait(dve, stored[c % 2], (P // QUAD) * DMA * (2 * b + c // 2))
                dve.transpose(z_t[:, c % 2], z_f[:, c % 2]).then_inc(z_t_made, 1)

            for j in (HG - 2, HG - 1):
                head(B - 1, C - 1, j)
            turn_x(0, 0)
            dve.wait_ge(bo_mm, 1)
            dve.wait_ge(small_landed, 4 * DMA)
            dve.tensor_tensor(bias_o[:, :], ps_score[0][:, 0:C], bo_col[:, :], ALU.add).then_inc(bo_made, 1)
            for n in range(4):
                one_over_den(B - 1, C - 1, n)
            normalize(B - 1, C - 1)
            dve.wait_ge(bo_made, 1)
            y_out(0, 0)
            w2_low(0)
            y_low(0, 0)
            for c in range(1, C):
                turn_x(0, c)
                y_out(0, c)
                if c == 2:
                    w2_low(1)
                y_low(0, c)
            expert_low(0, 0)

            def rows(b, first, last):
                for m in range(KH):
                    hidden_low(b, m)
                    if first and m < 2:
                        w2_low(2 + m)
                        expert_low(b, m + 1)
                    if m == 4:
                        expert_low(b, 3)
                    if first and 2 <= m < W2S - 2:
                        w2_low(2 + m)
                    if not last and m in (6, 10, 14):
                        expert_low(b + 1, m // 4 - 1)
                    if not last and 3 <= m < 3 + C:
                        attended_low(b + 1, m - 3)
                    if not last and m == KH - 4:
                        turn_x(b + 1, 0)
                        y_out(b + 1, 0)
                    if not last and m == KH - 2:
                        y_low(b + 1, 0)
                        turn_x(b + 1, 1)
                        y_out(b + 1, 1)
                if not last:
                    y_low(b + 1, 1)
                    for c in range(2, C):
                        turn_x(b + 1, c)
                        y_out(b + 1, c)
                        y_low(b + 1, c)
                for c in range(C):
                    turn_result(b, c)

            batches(dve, rows)

        @block.tensor
        def _(pe):
            def three(ps, left, right, first, last):
                pe.matmul(ps, left[0], right[0], start=first, stop=False)
                pe.matmul(ps, left[0], right[1], start=False, stop=False)
                return pe.matmul(ps, left[1], right[0], start=False, stop=last)

            def bias_products(w):
                for n in range(2):
                    pe.wait_ge(b_in_landed[n], DMA)
                pe.wait_ge(w_landed[w], DMA)
                for c in range(C):
                    at = 2 * c
                    for k in range(C):
                        mm = pe.matmul(ps_av[w][:, at:at + 2], w_raw[:, w, k, P * c:P * (c + 1)], b_in[:, k, :],
                                       start=(k == 0), stop=(k == C - 1))
                mm.then_inc(bias_mm, 1)

            def weight(w, k, c):
                at = slice(P * c, P * (c + 1))
                return w_hi[:, w, k, at], w_lo[:, w, k, at]

            def feature(s, k):
                return in_hi[:, s, k], in_lo[:, s, k]

            def project(b, c, n, third):
                G = C * b + c
                ps = ps_proj[n % 2][:, :]
                w, s, done = ((0, 0, q_mm), (1, 1, k_mm), (2, 0, v2_mm), (1, 0, k2_mm))[n]
                if third == 0:
                    if n == 0:
                        pe.wait_ge(in_lo_made, 2 * C * (b + 1))
                        wait(pe, v2_made, G)
                        if c == 2:
                            pe.wait_ge(v_lo_made, C * b + C)
                    if n == 1:
                        pe.wait_ge(in_lo_made, 2 * C * b + C)
                        wait(pe, qk_f_made, G)
                        if c == 2:
                            pe.wait_ge(v_lo_made, C * b + C - 1)
                    if n == 2:
                        pe.wait_ge(q_hi_made, G + 1)
                    if n == 3:
                        pe.wait_ge(k_lo_made, G + 1)
                m = 0
                for k in range(C):
                    (l_hi, l_lo), (r_hi, r_lo) = weight(w, k, c), feature(s, k)
                    for left, right in ((l_hi, r_hi), (l_hi, r_lo), (l_lo, r_hi)):
                        if m // C == third:
                            mm = pe.matmul(ps, left, right, start=(m == 0), stop=(m == 3 * C - 1))
                        m += 1
                if third == 2:
                    mm.then_inc(done, 1)

            def values(b, t):
                ps = ps_proj[1 - t % 2][:, :]
                if t == 0:
                    wait(pe, qk_f_made, C * b + 2)
                if t == 1:
                    wait(pe, v2_made, C * b + 2)
                if t >= 2:
                    pe.wait_ge(v_lo_made, C * b + t - 1)
                keys = slice(P * t, P * (t + 1))
                for k in range(C):
                    mm = three(ps, (in_hi[:, 1, k, keys], in_lo[:, 1, k, keys]), (w_hi[:, 2, k], w_lo[:, 2, k]),
                               k == 0, k == C - 1)
                mm.then_inc(v_mm, 1)

            def max_tile(b, c, n):
                G, r, j, t = C * b + c, c % 2, n // C, n % C
                if t == 0:
                    pe.wait_ge(stacked[r][j], stack_count(b, c))
                wait(pe, max_made, TILES * G + n - 1)
                if n == 0:
                    wait(pe, m_row_made, G)
                if n == 1:
                    wait(pe, ow_made, G)
                pe.matmul(ps_max[n % 2][:, :], q_st[0:KM, r, j, P * t:P * (t + 1)], k_st[0:KM, r, j, :],
                          start=True, stop=True).then_inc(max_mm, 1)

            def own_scores(b, c):
                G = C * b + c
                pe.wait_ge(qk_lo_made, G + 1)
                pe.wait_ge(max_made, TILES * (G + 1))
                pe.matmul(ps_max[1][0:HG, :], sum_heads[:, :], qk_hi[:, :], start=True, stop=False)
                pe.matmul(ps_max[1][0:HG, :], sum_heads[:, :], qk_lo[:, :], start=False, stop=True).then_inc(own_mm, 1)

            def turn_max(b, c):
                pe.wait_ge(max_made, TILES * (C * b + c + 1))
                for t in range(C):
                    mm = pe.matmul(ps_max[0][0:HG, P * t:P * (t + 1)], m_col[:, t, :], f(ident[:, :]), start=True, stop=True)
                mm.then_inc(turn_mm, 1)

            def own_less_max(b, c):
                G = C * b + c
                pe.wait_ge(own_made, G + 1)
                pe.wait_ge(m_lo_made, G + 1)
                ps = ps_max[1][:, :]
                pe.matmul(ps, sum_spread[:, :], qk_hi[:, :], start=True, stop=False)
                pe.matmul(ps, sum_spread[:, :], qk_lo[:, :], start=False, stop=False)
                pe.matmul(ps, spread[:, :], m_neg[:, :], start=False, stop=True).then_inc(ow_mm, 1)

            def score_tile(b, g, i):
                T, r, j, t = TILES * (C * b + g) + i, g % 2, i // C, i % C
                if i == 0:
                    pe.wait_ge(m_landed[r], 2 * DMA * (2 * b + g // 2 + 1))
                wait(pe, p_hi_made, T - 1)
                pe.matmul(ps_score[i % 2][:, :], k_st[0:KS, r, j, P * t:P * (t + 1)], q_st[0:KS, r, j, :],
                          start=True, stop=True).then_inc(score_mm, 1)

            def value_tile(b, g, i):
                T, j, t = TILES * (C * b + g) + i, i // C, i % C
                if g == 0 and j == 0:
                    pe.wait_ge(v_lo_made, C * b + t + 1)
                if t == 0:
                    wait(pe, num_made, HG * (C * b + g) + j - 1)
                pe.wait_ge(p_lo_made, T + 1)
                ps, v = ps_av[j % 2][0:3 * DH, :], v_st[:, t, HG * g + j, :]
                pe.matmul(ps, v, p_hi[:, i % 4], start=(t == 0), stop=False)
                pe.matmul(ps, v, p_lo[:, i % 4], start=False, stop=(t == C - 1)).then_inc(av_mm, 1)

            order = (1, 0, 3, 2)

            bias_products(1)
            for n, splits in zip(order, (1, 2, 2, 3)):
                if n == 0:
                    bias_products(0)
                pe.wait_ge(w_lo_made, C * splits)
                for third in range(3):
                    project(0, 0, n, third)
            for t in range(3 * C):
                project(0, 1, order[t // 3], t % 3)
                for n in first_max(t):
                    max_tile(0, 0, n)
            own_scores(0, 0)
            turn_max(0, 0)
            values(0, 0)
            values(0, 1)
            own_less_max(0, 0)
            values(0, 2)
            values(0, 3)

            def batch(b, first, last):
                for g in range(C):
                    nxt, nxt2 = after(b, g, 1), after(b, g, 2)
                    more = not (last and g >= 2)
                    bound = not (last and g == C - 1)
                    for i in range(TILES):
                        score_tile(b, g, i)
                        if bound:
                            for n in tiles_of_max(i):
                                max_tile(*nxt, n)
                        if i == LAG - 1 and not (first and g == 0):
                            value_tile(*after(b, g, -1), TILES - 1)
                        if g == 0 and not first and 1 <= i < 1 + C:
                            values(b, i - 1)
                        if more and i >= 4:
                            project(*nxt2, order[(i - 4) // 3], (i - 4) % 3)
                        if bound and i == 10:
                            own_scores(*nxt)
                            turn_max(*nxt)
                        if bound and i == 13:
                            own_less_max(*nxt)
                        if i >= LAG:
                            value_tile(b, g, i - LAG)
                        elif i < LAG - 1 and not (first and g == 0):
                            value_tile(*after(b, g, -1), TILES - LAG + i)

            batches(pe, batch)
            for i in range(TILES - LAG, TILES):
                value_tile(B - 1, C - 1, i)

            pe.wait_ge(small_landed, 4 * DMA)
            pe.wait_ge(wide_lo_made, WIDE)
            for c in range(C):
                for k in range(C):
                    for n, part in enumerate((wo_hi, wo_lo)):
                        mm = pe.matmul(ps_score[0][:, c:c + 1], f(part[:, k, P * c:P * (c + 1)]), bv_col[:, k:k + 1],
                                       start=(k == 0 and n == 0), stop=(k == C - 1 and n == 1))
            mm.then_inc(bo_mm, 1)

            def out_project(b, c):
                n = C * b + c
                pe.wait_ge(a_lo_made, C * (b + 1))
                wait(pe, y_f_made, n - 1)
                at = slice(P * c, P * (c + 1))
                for k in range(C):
                    mm = three(ps_proj[c % 2][:, :], (wo_hi[:, k, at], wo_lo[:, k, at]), (a_hi[:, k], a_lo[:, k]),
                               k == 0, k == C - 1)
                mm.then_inc(o_mm, 1)

            def hidden(b, m, ks):
                n = KH * b + m
                if ks[0] == 0:
                    wait(pe, h_hi_made, n - 1)
                at = slice(P * m, P * (m + 1))
                for k in ks:
                    if m < 2:
                        pe.wait_ge(y_lo_made, C * b + k + 1)
                    mm = three(ps_av[m % 2][:, :], (w1_hi[:, k, at], w1_lo[:, k, at]), (y_hi[:, k], y_lo[:, k]),
                               k == 0, k == C - 1)
                if ks[-1] == C - 1:
                    mm.then_inc(h_mm, 1)

            def residuals(b):
                for c in range(C):
                    wait(pe, z_made, C * (b - 1) + c + 1)
                    pe.matmul(ps_out[c][:, :], ident[:, :], y_hi[:, c], start=True, stop=False)
                    pe.matmul(ps_out[c][:, :], ident[:, :], y_lo[:, c], start=False, stop=False)

            def outputs(b, m, first):
                pe.wait_ge(h_lo_made, KH * b + m + 1)
                if first and m % 2 == 0:
                    pe.wait_ge(w2_lo_made, m // 2 + 1)
                for c in range(C):
                    at = slice(P * c, P * (c + 1))
                    left = (w2_hi[:, m, at], w2_lo[:, m, at]) if c < CS else (we_hi[:, m], we_lo[:, m])
                    if c == CS and m % 4 == 0:
                        pe.wait_ge(we_lo_made, 4 * b + m // 4 + 1)
                    mm = three(ps_out[c][:, :], left, (h_hi[:, m % 2], h_lo[:, m % 2]), False, m == KH - 1)
                mm.then_inc(out_mm, 1)

            pe.wait_ge(v2_made, C * B)
            pe.wait_ge(qk_f_made, C * B)
            for c in range(C):
                out_project(0, c)
            pe.wait_ge(num_made, HG * C * B)

            def rows(b, first, last):
                for m in range(2):
                    hidden(b, m, range(C - 1))
                for m in range(2):
                    hidden(b, m, range(C - 1, C))
                residuals(b)
                for m in range(KH):
                    if m + 2 < KH:
                        hidden(b, m + 2, range(C))
                    outputs(b, m, first)
                    if not last and m in (9, 11, 13, 14):
                        out_project(b + 1, {9: 0, 11: 1, 13: 2, 14: 3}[m])

            batches(pe, rows)


_INS = ['x', 'fside_BxSxS_0', 'itok_B_18_1004', 'itok_B_0_7', 'L0_cond_Wq', 'L0_cond_bq', 'L0_cond_Wk', 'L0_cond_bk',
        'L0_cond_Wv', 'L0_cond_bv', 'L0_cond_Wo', 'L0_cond_bo', 'L0_cond_b_prev', 'L0_cond_b_self',
        'L1_cond_W1', 'L1_cond_b1', 'L1_cond_W2', 'L1_cond_b2', 'L1_cond_We', 'L1_cond_be']


def kernel(**inputs):
    import numpy as _np
    import concourse.bacc as _bacc
    from concourse import mybir as _mybir
    from concourse.bass_utils import run_bass_kernel_spmd as _run

    nc = _bacc.Bacc("TRN2", target_bir_lowering=False, num_devices=1)
    arrays, args = {}, []
    for name in _INS:
        a = _np.ascontiguousarray(inputs[name])
        arrays[f"in_{name}_dram"] = a
        args.append(nc.dram_tensor(f"in_{name}_dram", a.shape, _mybir.dt.from_np(a.dtype), kind="ExternalInput").ap())
    out = nc.dram_tensor("out_dram", inputs["x"].shape, _mybir.dt.float32, kind="ExternalOutput").ap()
    cond_resid_program(nc, *args, out)
    r = _run(nc, [arrays], core_ids=[0])
    return r.results[0]["out_dram"]
```
